# Optimizing a Trainium2 kernel written in Bass

```python
import numpy as np
import jax
import jax.numpy as jnp

def _softmax(x, axis=-1):
    return jax.nn.softmax(x, axis=axis)

def _gelu(x):
    return jax.nn.gelu(x, approximate=True)

def _silu(x):
    return jax.nn.silu(x)

def _sigmoid(x):
    return jax.nn.sigmoid(x)

def _layernorm(x, axis=-1, eps=1e-05):
    m = jnp.mean(x, axis=axis, keepdims=True)
    v = jnp.var(x, axis=axis, keepdims=True)
    return (x - m) / jnp.sqrt(v + eps)

def _scatter_add(tgt, idx, src, axis=0):
    return tgt.at[idx].add(src)

def _segment_sum(src, seg, n):
    return jax.ops.segment_sum(src, seg, n)
kernel_name = 'mk_dlrm_tower_d1_rec_r8_46480a'

def setup_inputs(seed: int=0):
    np.random.seed(seed)
    _w = jnp.asarray

    def _rec_inputs():
        import jax
        import jax.numpy as jnp
        _tk = jax.random.key(seed)
        dense_ctx = jax.random.normal(jax.random.fold_in(_tk, 190), (1024, 16), jnp.float32)
        ids = jnp.stack([jax.random.randint(jax.random.fold_in(_tk, 200 + f), (1024,), 0, v, jnp.int32) for f, v in enumerate([12500, 1250, 1250, 1000, 125000, 1000, 12500, 125000, 1250, 12500, 1250, 125000, 1250, 1250, 1250, 1000, 12500, 12500, 1000, 1250, 1000, 1000, 1250, 12500, 12500, 12500, 1000, 1000, 1000, 1000, 1000, 1000])], axis=1)
        tbl_0 = 0.05 * jax.random.normal(jax.random.fold_in(_tk, 500 + 0), (12500, 64), jnp.float32)
        tbl_1 = 0.05 * jax.random.normal(jax.random.fold_in(_tk, 500 + 1), (1250, 64), jnp.float32)
        tbl_2 = 0.05 * jax.random.normal(jax.random.fold_in(_tk, 500 + 2), (1250, 64), jnp.float32)
        tbl_3 = 0.05 * jax.random.normal(jax.random.fold_in(_tk, 500 + 3), (1000, 64), jnp.float32)
        tbl_4 = 0.05 * jax.random.normal(jax.random.fold_in(_tk, 500 + 4), (125000, 64), jnp.float32)
        tbl_5 = 0.05 * jax.random.normal(jax.random.fold_in(_tk, 500 + 5), (1000, 64), jnp.float32)
        tbl_6 = 0.05 * jax.random.normal(jax.random.fold_in(_tk, 500 + 6), (12500, 64), jnp.float32)
        tbl_7 = 0.05 * jax.random.normal(jax.random.fold_in(_tk, 500 + 7), (125000, 64), jnp.float32)
        tbl_8 = 0.05 * jax.random.normal(jax.random.fold_in(_tk, 500 + 8), (1250, 64), jnp.float32)
        tbl_9 = 0.05 * jax.random.normal(jax.random.fold_in(_tk, 500 + 9), (12500, 64), jnp.float32)
        tbl_10 = 0.05 * jax.random.normal(jax.random.fold_in(_tk, 500 + 10), (1250, 64), jnp.float32)
        tbl_11 = 0.05 * jax.random.normal(jax.random.fold_in(_tk, 500 + 11), (125000, 64), jnp.float32)
        tbl_12 = 0.05 * jax.random.normal(jax.random.fold_in(_tk, 500 + 12), (1250, 64), jnp.float32)
        tbl_13 = 0.05 * jax.random.normal(jax.random.fold_in(_tk, 500 + 13), (1250, 64), jnp.float32)
        tbl_14 = 0.05 * jax.random.normal(jax.random.fold_in(_tk, 500 + 14), (1250, 64), jnp.float32)
        tbl_15 = 0.05 * jax.random.normal(jax.random.fold_in(_tk, 500 + 15), (1000, 64), jnp.float32)
        tbl_16 = 0.05 * jax.random.normal(jax.random.fold_in(_tk, 500 + 16), (12500, 64), jnp.float32)
        tbl_17 = 0.05 * jax.random.normal(jax.random.fold_in(_tk, 500 + 17), (12500, 64), jnp.float32)
        tbl_18 = 0.05 * jax.random.normal(jax.random.fold_in(_tk, 500 + 18), (1000, 64), jnp.float32)
        tbl_19 = 0.05 * jax.random.normal(jax.random.fold_in(_tk, 500 + 19), (1250, 64), jnp.float32)
        tbl_20 = 0.05 * jax.random.normal(jax.random.fold_in(_tk, 500 + 20), (1000, 64), jnp.float32)
        tbl_21 = 0.05 * jax.random.normal(jax.random.fold_in(_tk, 500 + 21), (1000, 64), jnp.float32)
        tbl_22 = 0.05 * jax.random.normal(jax.random.fold_in(_tk, 500 + 22), (1250, 64), jnp.float32)
        tbl_23 = 0.05 * jax.random.normal(jax.random.fold_in(_tk, 500 + 23), (12500, 64), jnp.float32)
        tbl_24 = 0.05 * jax.random.normal(jax.random.fold_in(_tk, 500 + 24), (12500, 64), jnp.float32)
        tbl_25 = 0.05 * jax.random.normal(jax.random.fold_in(_tk, 500 + 25), (12500, 64), jnp.float32)
        tbl_26 = 0.05 * jax.random.normal(jax.random.fold_in(_tk, 500 + 26), (1000, 64), jnp.float32)
        tbl_27 = 0.05 * jax.random.normal(jax.random.fold_in(_tk, 500 + 27), (1000, 64), jnp.float32)
        tbl_28 = 0.05 * jax.random.normal(jax.random.fold_in(_tk, 500 + 28), (1000, 64), jnp.float32)
        tbl_29 = 0.05 * jax.random.normal(jax.random.fold_in(_tk, 500 + 29), (1000, 64), jnp.float32)
        tbl_30 = 0.05 * jax.random.normal(jax.random.fold_in(_tk, 500 + 30), (1000, 64), jnp.float32)
        tbl_31 = 0.05 * jax.random.normal(jax.random.fold_in(_tk, 500 + 31), (1000, 64), jnp.float32)
        _rk = jax.random.fold_in(_tk, 7)
        W_top1 = 0.0606339 * jax.random.normal(jax.random.fold_in(_tk, 801), (272, 512), jnp.float32)
        W_top2 = 0.0441942 * jax.random.normal(jax.random.fold_in(_tk, 802), (512, 256), jnp.float32)
        W_top3 = 0.0625 * jax.random.normal(jax.random.fold_in(_tk, 803), (256, 1), jnp.float32)
        b_top1 = jnp.zeros((512,), jnp.float32)
        b_top2 = jnp.zeros((256,), jnp.float32)
        return (dense_ctx, ids, tbl_0, tbl_1, tbl_2, tbl_3, tbl_4, tbl_5, tbl_6, tbl_7, tbl_8, tbl_9, tbl_10, tbl_11, tbl_12, tbl_13, tbl_14, tbl_15, tbl_16, tbl_17, tbl_18, tbl_19, tbl_20, tbl_21, tbl_22, tbl_23, tbl_24, tbl_25, tbl_26, tbl_27, tbl_28, tbl_29, tbl_30, tbl_31, W_top1, b_top1, W_top2, b_top2, W_top3)
    dense_ctx, ids, tbl_0, tbl_1, tbl_2, tbl_3, tbl_4, tbl_5, tbl_6, tbl_7, tbl_8, tbl_9, tbl_10, tbl_11, tbl_12, tbl_13, tbl_14, tbl_15, tbl_16, tbl_17, tbl_18, tbl_19, tbl_20, tbl_21, tbl_22, tbl_23, tbl_24, tbl_25, tbl_26, tbl_27, tbl_28, tbl_29, tbl_30, tbl_31, W_top1, b_top1, W_top2, b_top2, W_top3 = _rec_inputs()

    def _L0_rec_setup():
        import jax, jax.numpy as jnp
        import numpy as np
        EMB_DIM = 64
        NUM_FIELDS = 32
        NUM_PAIRS = NUM_FIELDS * (NUM_FIELDS - 1) // 2
        D1 = 256
        BATCH = 256
        key = jax.random.key(seed)
        k1, k2, k3 = jax.random.split(key, 3)
        feat_emb = jax.random.normal(k1, (BATCH, NUM_FIELDS, EMB_DIM), dtype=jnp.float32)
        lim_k = float(np.sqrt(6.0 / (EMB_DIM + EMB_DIM)))
        kernel = jax.random.uniform(k2, (EMB_DIM, NUM_PAIRS, EMB_DIM), minval=-lim_k, maxval=lim_k, dtype=jnp.float32)
        lim_w = float(np.sqrt(6.0 / (NUM_PAIRS + D1)))
        W = jax.random.uniform(k3, (D1, NUM_PAIRS), minval=-lim_w, maxval=lim_w, dtype=jnp.float32)
        b = jnp.zeros((D1,), dtype=jnp.float32)
        return {'feat_emb': feat_emb, 'kernel': kernel, 'W': W, 'b': b}
    _L0_rec_all = _L0_rec_setup()
    _L0_rec_in = {k: v for k, v in _L0_rec_all.items() if k in ('kernel', 'W', 'b')}
    del _L0_rec_all
    return {'dense_ctx': dense_ctx, 'ids': ids, 'tbl_0': tbl_0, 'tbl_1': tbl_1, 'tbl_2': tbl_2, 'tbl_3': tbl_3, 'tbl_4': tbl_4, 'tbl_5': tbl_5, 'tbl_6': tbl_6, 'tbl_7': tbl_7, 'tbl_8': tbl_8, 'tbl_9': tbl_9, 'tbl_10': tbl_10, 'tbl_11': tbl_11, 'tbl_12': tbl_12, 'tbl_13': tbl_13, 'tbl_14': tbl_14, 'tbl_15': tbl_15, 'tbl_16': tbl_16, 'tbl_17': tbl_17, 'tbl_18': tbl_18, 'tbl_19': tbl_19, 'tbl_20': tbl_20, 'tbl_21': tbl_21, 'tbl_22': tbl_22, 'tbl_23': tbl_23, 'tbl_24': tbl_24, 'tbl_25': tbl_25, 'tbl_26': tbl_26, 'tbl_27': tbl_27, 'tbl_28': tbl_28, 'tbl_29': tbl_29, 'tbl_30': tbl_30, 'tbl_31': tbl_31, 'W_top1': W_top1, 'b_top1': b_top1, 'W_top2': W_top2, 'b_top2': b_top2, 'W_top3': W_top3, 'L0_rec_kernel': _L0_rec_in['kernel'], 'L0_rec_W': _L0_rec_in['W'], 'L0_rec_b': _L0_rec_in['b']}

def reference(dense_ctx, ids, tbl_0, tbl_1, tbl_2, tbl_3, tbl_4, tbl_5, tbl_6, tbl_7, tbl_8, tbl_9, tbl_10, tbl_11, tbl_12, tbl_13, tbl_14, tbl_15, tbl_16, tbl_17, tbl_18, tbl_19, tbl_20, tbl_21, tbl_22, tbl_23, tbl_24, tbl_25, tbl_26, tbl_27, tbl_28, tbl_29, tbl_30, tbl_31, W_top1, b_top1, W_top2, b_top2, W_top3, L0_rec_kernel, L0_rec_W, L0_rec_b):
    import jax
    import jax.numpy as jnp

    def _L0_rec_ref(feat_emb, kernel, W, b):
        import jax, jax.numpy as jnp
        import numpy as np
        EMB_DIM = 64
        NUM_FIELDS = 32
        NUM_PAIRS = NUM_FIELDS * (NUM_FIELDS - 1) // 2
        D1 = 256
        BATCH = 256
        num_fields = feat_emb.shape[1]
        rows, cols = np.triu_indices(num_fields, k=1)
        p = feat_emb[:, rows, :]
        q = feat_emb[:, cols, :]
        pij = jnp.einsum('bpe,dpe,bpd->bp', p, kernel, q)
        return pij @ W.T + b
    e = jnp.stack([tbl_0[ids[:, 0]], tbl_1[ids[:, 1]], tbl_2[ids[:, 2]], tbl_3[ids[:, 3]], tbl_4[ids[:, 4]], tbl_5[ids[:, 5]], tbl_6[ids[:, 6]], tbl_7[ids[:, 7]], tbl_8[ids[:, 8]], tbl_9[ids[:, 9]], tbl_10[ids[:, 10]], tbl_11[ids[:, 11]], tbl_12[ids[:, 12]], tbl_13[ids[:, 13]], tbl_14[ids[:, 14]], tbl_15[ids[:, 15]], tbl_16[ids[:, 16]], tbl_17[ids[:, 17]], tbl_18[ids[:, 18]], tbl_19[ids[:, 19]], tbl_20[ids[:, 20]], tbl_21[ids[:, 21]], tbl_22[ids[:, 22]], tbl_23[ids[:, 23]], tbl_24[ids[:, 24]], tbl_25[ids[:, 25]], tbl_26[ids[:, 26]], tbl_27[ids[:, 27]], tbl_28[ids[:, 28]], tbl_29[ids[:, 29]], tbl_30[ids[:, 30]], tbl_31[ids[:, 31]]], axis=1)
    z = _L0_rec_ref(e, L0_rec_kernel, L0_rec_W, L0_rec_b)
    z = z.reshape(z.shape[0], -1)
    h = jnp.concatenate([z, dense_ctx], axis=1)
    h = jnp.maximum(h @ W_top1 + b_top1, 0.0)
    h = jnp.maximum(h @ W_top2 + b_top2, 0.0)
    y = h @ W_top3
    return y

_drawn_inputs = setup_inputs


def setup_inputs(seed=0):
    import zlib

    import numpy as np

    out = dict(_drawn_inputs(seed))
    spreads = {'b_top1': (0.0, 0.1), 'b_top2': (0.0, 0.1), 'L0_rec_b': (0.0, 0.1)}
    factors = {'tbl_0': 3.356,
     'tbl_1': 3.174,
     'tbl_2': 3.356,
     'tbl_3': 3.325,
     'tbl_4': 3.454,
     'tbl_5': 3.337,
     'tbl_6': 3.108,
     'tbl_7': 3.159,
     'tbl_8': 3.43,
     'tbl_9': 3.12,
     'tbl_10': 3.376,
     'tbl_11': 3.193,
     'tbl_12': 3.195,
     'tbl_13': 3.442,
     'tbl_14': 3.006,
     'tbl_15': 3.218,
     'tbl_16': 3.392,
     'tbl_17': 3.02,
     'tbl_18': 3.317,
     'tbl_19': 2.957,
     'tbl_20': 3.088,
     'tbl_21': 3.475,
     'tbl_22': 3.534,
     'tbl_23': 2.956,
     'tbl_24': 3.425,
     'tbl_25': 3.14,
     'tbl_26': 3.193,
     'tbl_27': 3.393,
     'tbl_28': 3.53,
     'tbl_29': 3.19,
     'tbl_30': 3.284,
     'tbl_31': 3.372}
    for name, (base, spread) in spreads.items():
        noise = np.random.default_rng([zlib.crc32(name.encode()), seed]).standard_normal(out[name].shape)
        drawn = base * np.exp(spread * noise) if base else spread * noise
        out[name] = jnp.asarray(drawn.astype(out[name].dtype))
    for name, factor in factors.items():
        out[name] = (out[name] * factor).astype(out[name].dtype)
    return out
```

```python
import concourse.bass as bass
from concourse import mybir
from contextlib import ExitStack

EMB = 64
FIELDS = 32
BATCH = 1024
P = 128
HALF = 512
HALVES = BATCH // HALF
B_TILES = BATCH // P
FPAIRS = FIELDS // 2
DENSE = 16
Z_DIM, H1_DIM, H2_DIM = 256, 512, 256
H1_TILES, H2_TILES = H1_DIM // P, H2_DIM // P

UNITS = []
for _m in range(FPAIRS - 1, -1, -1):
    UNITS += [("full", _m, _n) for _n in range(_m + 1, FPAIRS)]
    if _m % 2 == 0:
        UNITS.append(("lone", _m))
UNITS_PER_STEP = 2
PAIR_STEPS = len(UNITS) // UNITS_PER_STEP
STEPS = PAIR_STEPS * HALVES
POSITIONS = 16
ROW_TILES = PAIR_STEPS // POSITIONS
ROWS = ROW_TILES * P
GROUP_UNITS = 4
GROUPS = len(UNITS) // GROUP_UNITS
GROUP_STEPS = GROUP_UNITS // UNITS_PER_STEP * HALVES
GROUP_COLS = GROUP_UNITS * 2 * P
KERNEL_SLOTS = 3
MOVING_SLOTS = 6
GATHER_SLOTS = 4
PRODUCT_SLOTS = 3
FIRST_POOL_GROUP = 22


def unit_fields(unit):
    if unit[0] == "full":
        return 2 * unit[1] + 1, 2 * unit[1]
    return 2 * unit[1], 2 * (unit[1] + 1)


def arrival(field):
    return FIELDS - 1 - field


def unit_row(u, chunk, parity):
    step = u // UNITS_PER_STEP
    group = 2 * (u % UNITS_PER_STEP) + chunk
    return step // POSITIONS, 32 * group + 2 * (step % POSITIONS) + parity


def row_of(u, chunk, parity):
    tile, row = unit_row(u, chunk, parity)
    return tile * P + row


def pair_index(i, j):
    return i * FIELDS - i * (i + 1) // 2 + (j - i - 1)


LONE_UNITS = [u for u, unit in enumerate(UNITS) if unit[0] == "lone"]


def first_step(m):
    return min(u for u, unit in enumerate(UNITS)
               if m in [f // 2 for f in unit_fields(unit)]) // UNITS_PER_STEP * HALVES


def field_plan():
    transposed = [[] for _ in range(STEPS)]
    split = [[] for _ in range(STEPS)]
    for m in range(FPAIRS - 1, -1, -1):
        need = first_step(m)
        if m > 10:
            order = [(need, need), (need, need)]
        else:
            order = [(need - 4, need - 3), (need - 3, need - 2)]
        for field, (t, s) in zip((2 * m + 1, 2 * m), order):
            transposed[t].append(field)
            split[s].append(field)
    return transposed, split


def dlrm_tower(nc, ids, tables, kernel_stream, w_rows, w_top1, b_rec, b_top1, w_top2, b_top2,
               w_top3, dense_t, identity, out):
    f32, f32r, i32 = mybir.dt.float32, mybir.dt.float32r, mybir.dt.int32
    ALU = mybir.AluOpType
    ACT = mybir.ActivationFunctionType
    transposed_at, split_at = field_plan()

    with ExitStack() as ctx:
        def sb(name, shape, dt=f32):
            return ctx.enter_context(nc.sbuf_tensor(name, shape, dt))

        def pb(name, shape):
            return ctx.enter_context(nc.psum_tensor(name, shape, f32))

        def sem(name):
            return ctx.enter_context(nc.semaphore(name))

        ids_sb = sb("ids_sb", [P, B_TILES * FIELDS], i32)
        gathered = sb("gathered", [P, GATHER_SLOTS, B_TILES, EMB])
        fields = sb("fields", [P, FPAIRS, BATCH])
        moving = sb("moving", [P, MOVING_SLOTS, BATCH], f32r)
        kernel_raw = sb("kernel_raw", [P, KERNEL_SLOTS, GROUP_COLS])
        kernel_high = sb("kernel_high", [P, KERNEL_SLOTS, GROUP_COLS], f32r)
        kernel_rest = sb("kernel_rest", [P, KERNEL_SLOTS, GROUP_COLS], f32r)
        products = sb("products", [P, PRODUCT_SLOTS, 2 * UNITS_PER_STEP, HALF])
        sums = sb("sums", [P, ROW_TILES, BATCH])
        w_rows_sb = sb("w_rows_sb", [P, 3, ROWS])
        w_top1_sb = sb("w_top1_sb", [P, 3, H1_DIM])
        w_head = sb("w_head", [P, ROW_TILES, H1_DIM])
        w_top2_sb = sb("w_top2_sb", [P, H1_TILES, H2_DIM])
        w_top3_sb = sb("w_top3_sb", [P, H2_TILES])
        b_rec_sb = sb("b_rec_sb", [P, Z_DIM // P])
        b_top1_sb = sb("b_top1_sb", [P, H1_TILES])
        b_head = sb("b_head", [P, H1_TILES])
        b_top2_sb = sb("b_top2_sb", [P, H2_TILES])
        identity_sb = sb("identity_sb", [P, P])
        selector = sb("selector", [P, 2 * (2 * POSITIONS) - 2])
        h1 = fields[:, 0:H1_TILES, :]
        h2 = fields[:, H1_TILES:H1_TILES + H2_TILES, :]
        y_row = fields[0:1, H1_TILES + H2_TILES, :]

        inner = [pb(f"inner{i}", [P, 2, HALF]) for i in range(UNITS_PER_STEP)]
        field_t = pb("field_t", [P, BATCH])
        row_sums = pb("row_sums", [P, HALVES, HALF])

        ids_loaded = sem("ids_loaded")
        weights_loaded = sem("weights_loaded")
        dense_loaded = sem("dense_loaded")
        sums_zeroed = sem("sums_zeroed")
        selector_zeroed = sem("selector_zeroed")
        selector_ready = sem("selector_ready")
        kernel_loaded = [sem(f"kernel_loaded{i}") for i in range(KERNEL_SLOTS)]
        kernel_high_ready = sem("kernel_high_ready")
        kernel_rest_ready = sem("kernel_rest_ready")
        field_gathered = [sem(f"field_gathered{i}") for i in range(GATHER_SLOTS)]
        field_transposed = sem("field_transposed")
        field_copied = sem("field_copied")
        field_split = sem("field_split")
        inner_ready = sem("inner_ready")
        product_ready = sem("product_ready")
        step_reduced = sem("step_reduced")
        sums_ready = sem("sums_ready")
        head_weights_made = sem("head_weights_made")
        head_weights_ready = sem("head_weights_ready")
        head_bias_made = sem("head_bias_made")
        head_bias_ready = sem("head_bias_ready")
        h1_made = sem("h1_made")
        h1_ready = sem("h1_ready")
        h2_made = sem("h2_made")
        h2_ready = sem("h2_ready")
        y_made = sem("y_made")
        y_ready = sem("y_ready")
        y_stored = sem("y_stored")

        def inner_count(step, q):
            return UNITS_PER_STEP * step + q + 1

        def last_inner_of_field(n):
            users = [u for u, unit in enumerate(UNITS) if FIELDS - 1 - n in unit_fields(unit)]
            if not users:
                return 0
            u = users[-1]
            return inner_count(u // UNITS_PER_STEP * HALVES + HALVES - 1, u % UNITS_PER_STEP)

        def closes_tile(step):
            return (step // HALVES) % POSITIONS == POSITIONS - 1

        def unit_of(step, q):
            return UNITS_PER_STEP * (step // HALVES) + q

        def h1_banks(half):
            if half == 0:
                return [inner[0][:, 0, :], inner[0][:, 1, :], inner[1][:, 0, :], inner[1][:, 1, :]]
            return [field_t[:, 0:HALF], field_t[:, HALF:BATCH], row_sums[:, 0, :], row_sums[:, 1, :]]

        def h2_banks(half):
            return [inner[half][:, 0, :], inner[half][:, 1, :]]

        def y_bank(half):
            return field_t[0:1, HALF * half:HALF * (half + 1)]

        block = ctx.enter_context(nc.Block())

        @block.sync
        def _(sp):
            def load_group(slot, group):
                for part in range(2):
                    sp.dma_start(kernel_raw[EMB * part:EMB * (part + 1), slot, :],
                                 kernel_stream[group, :, :]).then_inc(kernel_loaded[slot], 16)

            def load_group_at(slot, group):
                for part in range(2):
                    sp.dma_start(kernel_raw[EMB * part:EMB * (part + 1), slot, :],
                                 kernel_stream[bass.ds(group, 1), :, :].rearrange("g e c -> (g e) c")
                                 ).then_inc(kernel_loaded[slot], 16)

            sp.dma_start(ids_sb[:, :], ids).then_inc(ids_loaded, 16)
            sp.dma_start(identity_sb[:, :], identity).then_inc(weights_loaded, 16)
            for src, dst in ((w_rows, w_rows_sb), (w_top1, w_top1_sb)):
                sp.dma_start(dst[:, 0:2, :], src[0:Z_DIM, :].rearrange("(t p) c -> p t c", p=P)
                             ).then_inc(weights_loaded, 16)
                sp.dma_start(dst[0:DENSE, 2, :], src[Z_DIM:Z_DIM + DENSE, :]).then_inc(weights_loaded, 16)
            sp.dma_start(b_rec_sb[:, :], b_rec).then_inc(weights_loaded, 16)
            sp.dma_start(b_top1_sb[:, :], b_top1).then_inc(weights_loaded, 16)
            for slot in range(KERNEL_SLOTS):
                load_group(slot, slot)
            sp.dma_start(b_top2_sb[:, :], b_top2).then_inc(weights_loaded, 16)
            sp.dma_start(w_top3_sb[:, :], w_top3).then_inc(weights_loaded, 16)
            sp.dma_start(w_top2_sb[:, :, :], w_top2.rearrange("(t p) c -> p t c", p=P)).then_inc(weights_loaded, 16)
            sp.wait_ge(sums_zeroed, 1)
            for k, u in enumerate(LONE_UNITS):
                tile, row = unit_row(u, 0, 0)
                sp.dma_start(sums[row:row + 33:32, tile, :], dense_t[2 * k:2 * k + 2, :]
                             ).then_inc(dense_loaded, 16)
            looped = (GROUPS - KERNEL_SLOTS) // KERNEL_SLOTS * KERNEL_SLOTS
            with sp.Fori(KERNEL_SLOTS, KERNEL_SLOTS + looped, KERNEL_SLOTS) as group:
                for slot in range(KERNEL_SLOTS):
                    sp.wait_ge(kernel_rest_ready, group + (slot + 1 - KERNEL_SLOTS))
                    load_group_at(slot, group + slot)
            for group in range(KERNEL_SLOTS + looped, GROUPS):
                sp.wait_ge(kernel_rest_ready, group + 1 - KERNEL_SLOTS)
                load_group(group % KERNEL_SLOTS, group)
            sp.wait_ge(y_ready, HALVES)
            sp.dma_start(out.rearrange("b o -> o b"), y_row).then_inc(y_stored, 16)
            sp.wait_ge(y_stored, 16)

        @block.gpsimd
        def _(pool):
            pool.wait_ge(ids_loaded, 16)
            for n in range(FIELDS):
                field = FIELDS - 1 - n
                slot = n % GATHER_SLOTS
                if n >= GATHER_SLOTS:
                    pool.wait_ge(field_transposed, n + 1 - GATHER_SLOTS)
                for t in range(B_TILES):
                    column = t * FIELDS + field
                    nc.gpsimd.indirect_dma_start(
                        gathered[:, slot, t, :], None, tables[field],
                        bass.IndirectOffsetOnAxis(ap=ids_sb[:, column:column + 1], axis=0),
                    ).then_inc(field_gathered[slot], 16)
            pool.wait_ge(kernel_rest_ready, FIRST_POOL_GROUP)
            for group in range(FIRST_POOL_GROUP, GROUPS):
                slot = group % KERNEL_SLOTS
                pool.wait_ge(kernel_high_ready, group + 1)
                nc.gpsimd.tensor_tensor(kernel_rest[:, slot, :], kernel_raw[:, slot, :],
                                        kernel_high[:, slot, :].bitcast(f32), ALU.subtract
                                        ).then_inc(kernel_rest_ready, 1)

        @block.scalar
        def _(act):
            def kernel_group_high(group):
                slot = group % KERNEL_SLOTS
                act.wait_ge(kernel_loaded[slot], 32 * (group // KERNEL_SLOTS + 1))
                if group >= KERNEL_SLOTS:
                    act.wait_ge(inner_ready, inner_count(GROUP_STEPS * (group + 1 - KERNEL_SLOTS) - 1,
                                                         UNITS_PER_STEP - 1))
                nc.scalar.activation(kernel_high[:, slot, :], kernel_raw[:, slot, :], ACT.Copy
                                     ).then_inc(kernel_high_ready, 1)

            kernel_group_high(0)
            kernel_group_high(1)
            act.wait_ge(head_weights_made, 1)
            for q in range(UNITS_PER_STEP):
                last = nc.scalar.activation(w_head[:, 2 * q:2 * q + 2, :], inner[q][:, :, :], ACT.Copy)
            last.then_inc(head_weights_ready, 1)
            for step in range(STEPS):
                for field in transposed_at[step]:
                    n = arrival(field)
                    slot, half = n % MOVING_SLOTS, EMB * (field % 2)
                    act.wait_ge(field_transposed, n + 1)
                    if n >= MOVING_SLOTS and last_inner_of_field(n - MOVING_SLOTS):
                        act.wait_ge(inner_ready, last_inner_of_field(n - MOVING_SLOTS))
                    nc.scalar.activation(moving[0:EMB, slot, :], field_t[0:EMB, :], ACT.Copy)
                    nc.scalar.activation(fields[half:half + EMB, field // 2, :],
                                         field_t[0:EMB, :], ACT.Copy).then_inc(field_copied, 1)
                group = step // GROUP_STEPS + KERNEL_SLOTS - 1
                if step % GROUP_STEPS == 1 and group < GROUPS:
                    kernel_group_high(group)

            def relu_tiles(dst, banks, made, made_count, bias, ready, tiles, half):
                act.wait_ge(made, made_count)
                for t in range(tiles):
                    last = nc.scalar.activation(dst[:, t, HALF * half:HALF * (half + 1)], banks[t],
                                                ACT.Relu, bias=bias[:, t:t + 1])
                last.then_inc(ready, 1)

            act.wait_ge(head_bias_ready, 1)
            for half in range(HALVES):
                relu_tiles(h1, h1_banks(half), h1_made, half + 1, b_head, h1_ready, H1_TILES, half)
            for half in range(HALVES):
                relu_tiles(h2, h2_banks(half), h2_made, half + 1, b_top2_sb, h2_ready, H2_TILES, half)
            for half in range(HALVES):
                act.wait_ge(y_made, half + 1)
                nc.scalar.activation(y_row[:, HALF * half:HALF * (half + 1)], y_bank(half), ACT.Copy
                                     ).then_inc(y_ready, 1)

        @block.vector
        def _(dve):
            def kernel_group_rest(group):
                slot = group % KERNEL_SLOTS
                dve.wait_ge(kernel_high_ready, group + 1)
                nc.vector.tensor_tensor(kernel_rest[:, slot, :], kernel_raw[:, slot, :],
                                        kernel_high[:, slot, :].bitcast(f32), ALU.subtract
                                        ).then_inc(kernel_rest_ready, 1)

            def add_sums(step):
                tile, half = step // HALVES // POSITIONS, step % HALVES
                cols = slice(HALF * half, HALF * (half + 1))
                dve.wait_ge(step_reduced, step + 1)
                nc.vector.tensor_tensor(sums[:, tile, cols], row_sums[:, half, :], sums[:, tile, cols],
                                        ALU.add).then_inc(sums_ready, 1)

            nc.vector.memset(sums[:, :, :], 0.0).then_inc(sums_zeroed, 1)
            nc.vector.memset(selector[:, :], 0.0).then_inc(selector_zeroed, 1)
            dve.wait_ge(selector_zeroed, 1)
            nc.vector.memset(selector[0:EMB, 2 * POSITIONS - 2:2 * POSITIONS - 1], 1.0)
            nc.vector.memset(selector[EMB:P, 2 * POSITIONS - 1:2 * POSITIONS], 1.0).then_inc(selector_ready, 1)
            kernel_group_rest(0)
            kernel_group_rest(1)
            dve.wait_ge(head_bias_made, 1)
            nc.vector.tensor_tensor(b_head[:, :], field_t[:, 0:H1_TILES], b_top1_sb[:, :], ALU.add
                                    ).then_inc(head_bias_ready, 1)
            dve.wait_ge(dense_loaded, 16 * len(LONE_UNITS))
            for step in range(STEPS):
                for field in split_at[step]:
                    n = arrival(field)
                    slot = n % MOVING_SLOTS
                    dve.wait_ge(field_copied, n + 1)
                    nc.vector.tensor_tensor(moving[EMB:P, slot, :], field_t[0:EMB, :],
                                            moving[0:EMB, slot, :].bitcast(f32), ALU.subtract
                                            ).then_inc(field_split, 1)
                half = step % HALVES
                cols = slice(HALF * half, HALF * (half + 1))
                for q in range(UNITS_PER_STEP):
                    unit = UNITS[unit_of(step, q)]
                    dst = products[:, step % PRODUCT_SLOTS, 2 * q:2 * q + 2, :]
                    dve.wait_ge(inner_ready, inner_count(step, q))
                    if q == 0 and step >= PRODUCT_SLOTS:
                        dve.wait_ge(step_reduced, step + 1 - PRODUCT_SLOTS)
                    if unit[0] == "full":
                        dve.wait_ge(field_copied, arrival(2 * (unit[1] + 1)) + 1)
                        second = fields[:, unit[2]:unit[2] + 1, cols].to_broadcast([P, 2, HALF])
                        nc.vector.tensor_tensor(dst, inner[q][:, :, :], second, ALU.mult
                                                ).then_inc(product_ready, 1)
                    else:
                        dve.wait_ge(field_copied, arrival(2 * unit[1] + 1) + 1)
                        nc.vector.tensor_tensor(dst[EMB:P], inner[q][EMB:P, :, :],
                                                fields[EMB:P, unit[1]:unit[1] + 2, cols], ALU.mult
                                                ).then_inc(product_ready, 1)
                    if q == 0 and step >= 2 and closes_tile(step - 2):
                        add_sums(step - 2)
                group = step // GROUP_STEPS + KERNEL_SLOTS - 1
                if step % GROUP_STEPS == 1 and group < FIRST_POOL_GROUP:
                    kernel_group_rest(group)
            add_sums(STEPS - 2)
            add_sums(STEPS - 1)

        @block.tensor
        def _(pe):
            matmul = nc.tensor.matmul

            def reduce(step):
                tile_step, half = step // HALVES, step % HALVES
                position = tile_step % POSITIONS
                columns = selector[:, 2 * (POSITIONS - 1 - position):][:, 0:2 * POSITIONS]
                if position == 0 and tile_step >= POSITIONS:
                    pe.wait_ge(sums_ready, HALVES * (tile_step // POSITIONS - 1) + half + 1)
                pe.wait_ge(product_ready, UNITS_PER_STEP * (step + 1))
                for q in range(UNITS_PER_STEP):
                    rows = slice(0, P) if UNITS[unit_of(step, q)][0] == "full" else slice(EMB, P)
                    for chunk in range(2):
                        s = 2 * q + chunk
                        last = matmul(row_sums[32 * s:32 * s + 32, half, :], columns[rows],
                                      products[rows, step % PRODUCT_SLOTS, s, :],
                                      start=position == 0, stop=position == POSITIONS - 1,
                                      tile_position=(rows.start, 32 * s))
                last.then_inc(step_reduced, 1)

            pe.wait_ge(weights_loaded, 16 * 10)
            parts = ((0, P), (1, P), (2, DENSE))
            for tile in range(ROW_TILES):
                for part, rows in parts:
                    last = matmul(inner[tile // 2][:, tile % 2, :],
                                  w_rows_sb[0:rows, part, P * tile:P * (tile + 1)],
                                  w_top1_sb[0:rows, part, :], start=part == 0, stop=part == 2)
            last.then_inc(head_weights_made, 1)
            for t in range(H1_TILES):
                for part in range(2):
                    last = matmul(field_t[:, t:t + 1], w_top1_sb[:, part, P * t:P * (t + 1)],
                                  b_rec_sb[:, part:part + 1], start=part == 0, stop=part == 1)
            last.then_inc(head_bias_made, 1)
            pe.wait_ge(head_weights_ready, 1)
            pe.wait_ge(head_bias_ready, 1)
            pe.wait_ge(selector_ready, 1)
            for step in range(STEPS):
                for field in transposed_at[step]:
                    n = arrival(field)
                    slot = n % GATHER_SLOTS
                    pe.wait_ge(field_gathered[slot], 16 * B_TILES * (n // GATHER_SLOTS + 1))
                    if n > 0:
                        pe.wait_ge(field_split, n)
                    for t in range(B_TILES):
                        last = nc.tensor.transpose(field_t[0:EMB, P * t:P * (t + 1)], gathered[:, slot, t, :],
                                                   identity_sb[:, :])
                    last.then_inc(field_transposed, 1)
                half = step % HALVES
                cols = slice(HALF * half, HALF * (half + 1))
                for q in range(UNITS_PER_STEP):
                    u = unit_of(step, q)
                    group = u // GROUP_UNITS
                    kslot = group % KERNEL_SLOTS
                    pe.wait_ge(kernel_rest_ready, group + 1)
                    pe.wait_ge(field_split, max(arrival(f) for f in unit_fields(UNITS[u])) + 1)
                    if step > 0:
                        pe.wait_ge(product_ready, UNITS_PER_STEP * (step - 1) + q + 1)
                    for chunk in range(2):
                        mslot = arrival(unit_fields(UNITS[u])[chunk]) % MOVING_SLOTS
                        at = (2 * (u % GROUP_UNITS) + chunk) * P
                        for part, kernel_part in enumerate((kernel_high, kernel_rest)):
                            last = matmul(inner[q][:, chunk, :], kernel_part[:, kslot, at:at + P],
                                          moving[:, mslot, cols], start=part == 0, stop=part == 1)
                    last.then_inc(inner_ready, 1)
                if step > 0:
                    reduce(step - 1)
            reduce(STEPS - 1)

            pe.wait_ge(weights_loaded, 16 * 10)
            pe.wait_ge(product_ready, UNITS_PER_STEP * STEPS)
            for half in range(HALVES):
                cols = slice(HALF * half, HALF * (half + 1))
                for tile in range(ROW_TILES):
                    if half == 1 or tile == ROW_TILES - 1:
                        pe.wait_ge(sums_ready, HALVES * (ROW_TILES - 1) + (HALVES if half else 1))
                    for t in range(H1_TILES):
                        last = matmul(h1_banks(half)[t], w_head[:, tile, P * t:P * (t + 1)],
                                      sums[:, tile, cols], start=tile == 0, stop=tile == ROW_TILES - 1)
                last.then_inc(h1_made, 1)
            for half in range(HALVES):
                cols = slice(HALF * half, HALF * (half + 1))
                pe.wait_ge(h1_ready, half + 1)
                for t in range(H2_TILES):
                    for part in range(H1_TILES):
                        last = matmul(h2_banks(half)[t], w_top2_sb[:, part, P * t:P * (t + 1)],
                                      h1[:, part, cols], start=part == 0, stop=part == H1_TILES - 1)
                last.then_inc(h2_made, 1)
            for half in range(HALVES):
                cols = slice(HALF * half, HALF * (half + 1))
                pe.wait_ge(h2_ready, half + 1)
                for part in range(H2_TILES):
                    last = matmul(y_bank(half), w_top3_sb[:, part:part + 1], h2[:, part, cols],
                                  start=part == 0, stop=part == H2_TILES - 1)
                last.then_inc(y_made, 1)


def lay_out(inputs):
    import numpy as np

    arrays = {}
    ids = np.asarray(inputs["ids"])
    arrays["ids"] = np.ascontiguousarray(
        ids.reshape(B_TILES, P, FIELDS).transpose(1, 0, 2).reshape(P, B_TILES * FIELDS))
    for f in range(FIELDS):
        arrays[f"tbl_{f}"] = np.ascontiguousarray(inputs[f"tbl_{f}"])
    by_pair = np.asarray(inputs["L0_rec_kernel"]).transpose(1, 2, 0)
    w = np.asarray(inputs["L0_rec_W"])
    stream = np.empty((len(UNITS), 2, 2, EMB, EMB), by_pair.dtype)
    w_rows = np.zeros((Z_DIM + DENSE, ROWS), w.dtype)
    for u, unit in enumerate(UNITS):
        for chunk, field in enumerate(unit_fields(unit)):
            for parity in range(2):
                second = 2 * unit[2] + parity if unit[0] == "full" else field + 1
                p = pair_index(field, second)
                stream[u, chunk, parity] = by_pair[p]
                if unit[0] == "full" or parity == 1:
                    w_rows[:Z_DIM, row_of(u, chunk, parity)] = w[:, p]
    for k, u in enumerate(LONE_UNITS):
        for chunk in range(2):
            w_rows[Z_DIM + 2 * k + chunk, row_of(u, chunk, 0)] = 1
    arrays["kernel_stream"] = np.ascontiguousarray(
        stream.reshape(GROUPS, GROUP_UNITS * 4, EMB, EMB).transpose(0, 2, 1, 3).reshape(GROUPS, EMB, GROUP_COLS))
    arrays["w_rows"] = w_rows
    arrays["w_top1"] = np.ascontiguousarray(inputs["W_top1"])
    arrays["b_rec"] = np.ascontiguousarray(np.asarray(inputs["L0_rec_b"]).reshape(-1, P).T)
    arrays["b_top1"] = np.ascontiguousarray(np.asarray(inputs["b_top1"]).reshape(-1, P).T)
    arrays["w_top2"] = np.ascontiguousarray(inputs["W_top2"])
    arrays["b_top2"] = np.ascontiguousarray(np.asarray(inputs["b_top2"]).reshape(-1, P).T)
    arrays["w_top3"] = np.ascontiguousarray(np.asarray(inputs["W_top3"]).reshape(-1, P).T)
    arrays["dense_t"] = np.ascontiguousarray(np.asarray(inputs["dense_ctx"]).T)
    arrays["identity"] = np.eye(P, dtype=np.float32)
    return arrays


def kernel(**inputs):
    import numpy as np
    import concourse.bacc as bacc
    from concourse.bass_utils import run_bass_kernel_spmd

    nc = bacc.Bacc("TRN2", target_bir_lowering=False, num_devices=1)
    arrays, aps = {}, {}
    for name, a in lay_out(inputs).items():
        arrays[f"in_{name}"] = a
        aps[name] = nc.dram_tensor(f"in_{name}", a.shape, mybir.dt.from_np(a.dtype), kind="ExternalInput").ap()
    out = nc.dram_tensor("out_y", (BATCH, 1), mybir.dt.float32, kind="ExternalOutput").ap()
    tables = [aps.pop(f"tbl_{f}") for f in range(FIELDS)]
    dlrm_tower(nc, aps.pop("ids"), tables, out=out, **aps)
    return run_bass_kernel_spmd(nc, [arrays], core_ids=[0]).results[0]["out_y"]
```

```python
import concourse.bass as bass
from concourse import mybir
from contextlib import ExitStack

EMB = 64
FIELDS = 32
BATCH = 1024
P = 128
HALF = 512
HALVES = BATCH // HALF
B_TILES = BATCH // P
FPAIRS = FIELDS // 2
DENSE = 16
Z_DIM, H1_DIM, H2_DIM = 256, 512, 256
H1_TILES, H2_TILES = H1_DIM // P, H2_DIM // P

PAIR_ORDER = (15, 14, 13, 10, 9, 7, 12, 11, 8, 6, 5, 4, 3, 2, 1, 0)
ONE_HOT_FIELDS = (31, 29, 27)
ONE_HOT_ROWS = 1000
ONE_HOT_TILES = 8
ONE_HOT_PARTS = ONE_HOT_ROWS // ONE_HOT_TILES
ONE_HOT_SLOTS = 4
FIELD_ORDER = [f for m in PAIR_ORDER
               for f in sorted((2 * m, 2 * m + 1), key=lambda f: f not in ONE_HOT_FIELDS)]
GATHERED_FIELDS = [f for f in FIELD_ORDER if f not in ONE_HOT_FIELDS]

UNITS = []
for _at, _m in enumerate(PAIR_ORDER):
    UNITS += [("full", _m, _n) for _n in PAIR_ORDER[:_at]]
    if _at % 2 == 1:
        UNITS.append(("lone", *sorted(PAIR_ORDER[_at - 1:_at + 1])))
UNITS_PER_STEP = 2
PAIR_STEPS = len(UNITS) // UNITS_PER_STEP
STEPS = PAIR_STEPS * HALVES
POSITIONS = 16
ROW_TILES = PAIR_STEPS // POSITIONS
ROWS = ROW_TILES * P
GROUP_UNITS = 4
GROUPS = len(UNITS) // GROUP_UNITS
GROUP_STEPS = GROUP_UNITS // UNITS_PER_STEP * HALVES
GROUP_COLS = GROUP_UNITS * 2 * P
KERNEL_SLOTS = 3
MOVING_SLOTS = 6
EARLY_PAIRS = 4
GATHER_SLOTS = 4
PRODUCT_SLOTS = 2
FIRST_POOL_GROUP = 6


def unit_fields(unit):
    if unit[0] == "full":
        return 2 * unit[1] + 1, 2 * unit[1]
    return 2 * unit[1], 2 * unit[2]


def arrival(field):
    return FIELD_ORDER.index(field)


def unit_row(u, chunk, parity):
    step = u // UNITS_PER_STEP
    group = 2 * (u % UNITS_PER_STEP) + chunk
    return step // POSITIONS, 32 * group + 2 * (step % POSITIONS) + parity


def row_of(u, chunk, parity):
    tile, row = unit_row(u, chunk, parity)
    return tile * P + row


def pair_index(i, j):
    i, j = min(i, j), max(i, j)
    return i * FIELDS - i * (i + 1) // 2 + (j - i - 1)


HEAD_STEP = 2

LONE_UNITS = [u for u, unit in enumerate(UNITS) if unit[0] == "lone"]


def first_step(m):
    return min(u for u, unit in enumerate(UNITS) if m in unit[1:]) // UNITS_PER_STEP * HALVES


EARLY_AHEAD = {"prepare": 3, "take 0": 3, "take 1": 3, "split 0": 2, "split 1": 1,
               "take": 0, "split 2": 0, "split 3": 0}
LATE_AHEAD = {"prepare": 9, "take 0": 8, "take 1": 7, "split 0": 6, "split 1": 5,
              "take": 4, "split 2": 3, "split 3": 2}


def field_plan():
    events = [[] for _ in range(STEPS)]
    step = 0
    for at, m in enumerate(PAIR_ORDER):
        first, second = FIELD_ORDER[2 * at:2 * at + 2]
        looked_up = first in ONE_HOT_FIELDS
        ahead = EARLY_AHEAD if at < EARLY_PAIRS else LATE_AHEAD
        for name, event in (("prepare", ("prepare", first, 0)), ("take 0", ("take", first, 0)),
                            ("take 0", ("prepare", first, 1)), ("take 1", ("take", first, 1)),
                            ("split 0", ("split", first, 0)), ("split 1", ("split", first, 1)),
                            ("take", ("take", second, 1)),
                            ("split 2", ("split", second, 0)), ("split 3", ("split", second, 1))):
            if looked_up or (event[0] != "prepare" and name != "take 0"):
                step = max(step, first_step(m) - ahead[name])
                events[step].append(event)
    return events


def dlrm_tower(nc, ids, ids_t, one_hot_row, tables, kernel_stream, w_rows, w_top1, b_rec, b_top1, w_top2, b_top2,
               w_top3, dense_t, identity, out):
    f32, f32r, i32 = mybir.dt.float32, mybir.dt.float32r, mybir.dt.int32
    ALU = mybir.AluOpType
    ACT = mybir.ActivationFunctionType
    field_events = field_plan()

    with ExitStack() as ctx:
        def sb(name, shape, dt=f32):
            return ctx.enter_context(nc.sbuf_tensor(name, shape, dt))

        def pb(name, shape):
            return ctx.enter_context(nc.psum_tensor(name, shape, f32))

        def sem(name):
            return ctx.enter_context(nc.semaphore(name))

        ids_sb = sb("ids_sb", [P, B_TILES * FIELDS], i32)
        gathered = sb("gathered", [P, GATHER_SLOTS, B_TILES, EMB])
        fields = sb("fields", [P, FPAIRS, BATCH])
        moving = sb("moving", [P, MOVING_SLOTS, BATCH], f32r)
        kernel_raw = sb("kernel_raw", [P, KERNEL_SLOTS, GROUP_COLS])
        kernel_high = sb("kernel_high", [P, KERNEL_SLOTS, GROUP_COLS], f32r)
        kernel_rest = sb("kernel_rest", [P, KERNEL_SLOTS, GROUP_COLS], f32r)
        products = sb("products", [P, PRODUCT_SLOTS, 2 * UNITS_PER_STEP, HALF])
        sums = sb("sums", [P, ROW_TILES, BATCH])
        w_head = sb("w_head", [P, ROW_TILES, H1_DIM])
        w_top2_sb = sb("w_top2_sb", [P, H1_TILES, H2_DIM])
        w_top3_sb = sb("w_top3_sb", [P, H2_TILES])
        b_rec_sb = sb("b_rec_sb", [P, Z_DIM // P])
        b_top1_sb = sb("b_top1_sb", [P, H1_TILES])
        b_head = sb("b_head", [P, H1_TILES])
        b_top2_sb = sb("b_top2_sb", [P, H2_TILES])
        identity_sb = sb("identity_sb", [P, P])
        tables_sb = sb("tables_sb", [P, 4, ONE_HOT_TILES, EMB])
        one_hot_row_sb = sb("one_hot_row_sb", [P, ONE_HOT_TILES])
        one_hot = sb("one_hot", [P, ONE_HOT_SLOTS, BATCH], f32r)
        table_parts = sb("table_parts", [P, ONE_HOT_TILES, 2 * EMB], f32r)
        selector = sb("selector", [P, 2 * (2 * POSITIONS) - 2])
        w_rows_sb = fields[:, 0:2, :].rearrange("p a (b c) -> p (a b) c", c=ROWS)[:, 0:3, :]
        w_top1_sb = fields[:, 1:3, :].rearrange("p a (b c) -> p (a b) c", c=H1_DIM)[:, 1:4, :]
        lookup_ids = [fields[:, m, :].bitcast(i32) for m in (4, 5, 6, 8, 11, 12)]
        spare_tables = fields[:, 3, :].rearrange("p (a k e) -> p a k e", k=ONE_HOT_TILES, e=EMB)
        lookup_tables = [tables_sb[:, k, :, :] for k in range(4)] + [spare_tables[:, k, :, :] for k in range(2)]
        h1 = fields[:, 0:H1_TILES, :]
        h2 = fields[:, H1_TILES:H1_TILES + H2_TILES, :]
        y_row = fields[0:1, H1_TILES + H2_TILES, :]

        inner = [pb(f"inner{i}", [P, 2, HALF]) for i in range(UNITS_PER_STEP)]
        field_t = pb("field_t", [P, BATCH])
        row_sums = pb("row_sums", [P, HALVES, HALF])

        ids_loaded = sem("ids_loaded")
        identity_loaded = sem("identity_loaded")
        weights_loaded = sem("weights_loaded")
        dense_loaded = sem("dense_loaded")
        sums_zeroed = sem("sums_zeroed")
        selector_zeroed = sem("selector_zeroed")
        selector_ready = sem("selector_ready")
        kernel_loaded = [sem(f"kernel_loaded{i}") for i in range(KERNEL_SLOTS)]
        kernel_high_ready = sem("kernel_high_ready")
        kernel_rest_ready = sem("kernel_rest_ready")
        field_gathered = [sem(f"field_gathered{i}") for i in range(GATHER_SLOTS)]
        lookup_rows_loaded = sem("lookup_rows_loaded")
        lookup_loaded = [sem(f"lookup_loaded{f}") for f in ONE_HOT_FIELDS]
        table_high_ready = sem("table_high_ready")
        table_rest_ready = sem("table_rest_ready")
        one_hot_made = sem("one_hot_made")
        one_hot_used = sem("one_hot_used")
        field_transposed = sem("field_transposed")
        field_copied = sem("field_copied")
        field_split = sem("field_split")
        inner_ready = sem("inner_ready")
        product_ready = sem("product_ready")
        step_reduced = sem("step_reduced")
        sums_ready = sem("sums_ready")
        head_weights_made = sem("head_weights_made")
        head_weights_ready = sem("head_weights_ready")
        head_bias_made = sem("head_bias_made")
        head_bias_ready = sem("head_bias_ready")
        h1_made = sem("h1_made")
        h1_ready = sem("h1_ready")
        h2_made = sem("h2_made")
        h2_ready = sem("h2_ready")
        y_made = sem("y_made")
        y_ready = sem("y_ready")
        y_stored = sem("y_stored")

        def inner_count(step, q):
            return UNITS_PER_STEP * step + q + 1

        def last_inner_of_field(n):
            users = [u for u, unit in enumerate(UNITS) if FIELD_ORDER[n] in unit_fields(unit)]
            if not users:
                return 0
            u = users[-1]
            return inner_count(u // UNITS_PER_STEP * HALVES + HALVES - 1, u % UNITS_PER_STEP)

        def closes_tile(step):
            return (step // HALVES) % POSITIONS == POSITIONS - 1

        def group_made_at(step):
            group = step // GROUP_STEPS + KERNEL_SLOTS - 1
            return group if step % GROUP_STEPS == 1 and group < GROUPS else None

        def unit_of(step, q):
            return UNITS_PER_STEP * (step // HALVES) + q

        def by_tiles(row, odd):
            return row.rearrange("p (t odd b) -> p odd t b", odd=2, b=P)[:, odd, :, :]

        def transposed(n):
            return field_t[:, HALF * (n % 2):HALF * (n % 2 + 1)]

        def transposed_tiles(n, odd):
            return transposed(n)[EMB * odd:EMB * (odd + 1), :].rearrange("p (t b) -> p t b", b=P)

        def bank_holder(n):
            both = FIELD_ORDER[n] in ONE_HOT_FIELDS or FIELD_ORDER[n - 1] in ONE_HOT_FIELDS
            return n if both else n - 1

        def h1_banks(half):
            if half == 0:
                return [inner[0][:, 0, :], inner[0][:, 1, :], inner[1][:, 0, :], inner[1][:, 1, :]]
            return [field_t[:, 0:HALF], field_t[:, HALF:BATCH], row_sums[:, 0, :], row_sums[:, 1, :]]

        def h2_banks(half):
            return [inner[half][:, 0, :], inner[half][:, 1, :]]

        def y_part(quarter):
            return field_t[32 * quarter:32 * quarter + 1, 0:BATCH // 4]

        block = ctx.enter_context(nc.Block())

        @block.sync
        def _(sp):
            def load_group(slot, group):
                for part in range(2):
                    sp.dma_start(kernel_raw[EMB * part:EMB * (part + 1), slot, :],
                                 kernel_stream[group, :, :]).then_inc(kernel_loaded[slot], 16)

            def load_group_at(slot, group):
                for part in range(2):
                    sp.dma_start(kernel_raw[EMB * part:EMB * (part + 1), slot, :],
                                 kernel_stream[bass.ds(group, 1), :, :].rearrange("g e c -> (g e) c")
                                 ).then_inc(kernel_loaded[slot], 16)

            def load_lookup(k):
                field = ONE_HOT_FIELDS[k]
                sp.dma_start(lookup_tables[k][0:ONE_HOT_PARTS],
                             tables[field].rearrange("(p k) e -> p k e", k=ONE_HOT_TILES)
                             ).then_inc(lookup_loaded[k], 16)
                sp.dma_start(lookup_ids[k], ids_t[field:field + 1, :].to_broadcast([P, BATCH])
                             ).then_inc(lookup_loaded[k], 16)

            sp.dma_start(ids_sb[:, :], ids).then_inc(ids_loaded, 16)
            sp.dma_start(one_hot_row_sb[0:ONE_HOT_PARTS, :], one_hot_row).then_inc(lookup_rows_loaded, 16)
            load_lookup(0)
            sp.dma_start(identity_sb[:, :], identity).then_inc(identity_loaded, 16)
            load_lookup(1)
            load_group(0, 0)
            load_group(1, 1)
            for src, dst in ((w_rows, w_rows_sb), (w_top1, w_top1_sb)):
                sp.dma_start(dst[:, 0:2, :], src[0:Z_DIM, :].rearrange("(t p) c -> p t c", p=P)
                             ).then_inc(weights_loaded, 16)
                sp.dma_start(dst[0:DENSE, 2, :], src[Z_DIM:Z_DIM + DENSE, :]).then_inc(weights_loaded, 16)
            sp.dma_start(b_rec_sb[:, :], b_rec).then_inc(weights_loaded, 16)
            sp.dma_start(b_top1_sb[:, :], b_top1).then_inc(weights_loaded, 16)
            for k in range(2, len(ONE_HOT_FIELDS)):
                load_lookup(k)
            load_group(2, 2)
            sp.dma_start(b_top2_sb[:, :], b_top2).then_inc(weights_loaded, 16)
            sp.dma_start(w_top3_sb[:, :], w_top3).then_inc(weights_loaded, 16)
            sp.dma_start(w_top2_sb[:, :, :], w_top2.rearrange("(t p) c -> p t c", p=P)).then_inc(weights_loaded, 16)
            sp.wait_ge(sums_zeroed, 1)
            for k, u in enumerate(LONE_UNITS):
                tile, row = unit_row(u, 0, 0)
                sp.dma_start(sums[row:row + 33:32, tile, :], dense_t[2 * k:2 * k + 2, :]
                             ).then_inc(dense_loaded, 16)
            looped = (GROUPS - KERNEL_SLOTS) // KERNEL_SLOTS * KERNEL_SLOTS
            with sp.Fori(KERNEL_SLOTS, KERNEL_SLOTS + looped, KERNEL_SLOTS) as group:
                for slot in range(KERNEL_SLOTS):
                    sp.wait_ge(kernel_rest_ready, group + (slot + 1 - KERNEL_SLOTS))
                    load_group_at(slot, group + slot)
            for group in range(KERNEL_SLOTS + looped, GROUPS):
                sp.wait_ge(kernel_rest_ready, group + 1 - KERNEL_SLOTS)
                load_group(group % KERNEL_SLOTS, group)
            sp.wait_ge(y_ready, 1)
            sp.dma_start(out.rearrange("b o -> o b"), y_row).then_inc(y_stored, 16)
            sp.wait_ge(y_stored, 16)

        @block.gpsimd
        def _(pool):
            def gather_field(n):
                field = GATHERED_FIELDS[n]
                slot = n % GATHER_SLOTS
                if n >= GATHER_SLOTS:
                    pool.wait_ge(field_transposed, arrival(GATHERED_FIELDS[n - GATHER_SLOTS]) + 1)
                for t in range(B_TILES):
                    column = t * FIELDS + field
                    nc.gpsimd.indirect_dma_start(
                        gathered[:, slot, t, :], None, tables[field],
                        bass.IndirectOffsetOnAxis(ap=ids_sb[:, column:column + 1], axis=0),
                    ).then_inc(field_gathered[slot], 16)

            def kernel_group_rest(group):
                slot = group % KERNEL_SLOTS
                pool.wait_ge(kernel_high_ready, group + 1)
                nc.gpsimd.tensor_tensor(kernel_rest[:, slot, :], kernel_raw[:, slot, :],
                                        kernel_high[:, slot, :].bitcast(f32), ALU.subtract
                                        ).then_inc(kernel_rest_ready, 1)

            pool.wait_ge(ids_loaded, 16)
            n = taken = 0
            for step in range(STEPS):
                taken += sum(e[0] == "take" and e[1] in GATHERED_FIELDS for e in field_events[step])
                while n < min(taken + GATHER_SLOTS, len(GATHERED_FIELDS)):
                    gather_field(n)
                    n += 1
                group = group_made_at(step)
                if group is not None and group >= FIRST_POOL_GROUP:
                    if group == FIRST_POOL_GROUP:
                        pool.wait_ge(kernel_rest_ready, FIRST_POOL_GROUP)
                    kernel_group_rest(group)

        @block.scalar
        def _(act):
            def kernel_group_high(group):
                slot = group % KERNEL_SLOTS
                act.wait_ge(kernel_loaded[slot], 32 * (group // KERNEL_SLOTS + 1))
                if group >= KERNEL_SLOTS:
                    act.wait_ge(inner_ready, inner_count(GROUP_STEPS * (group + 1 - KERNEL_SLOTS) - 1,
                                                         UNITS_PER_STEP - 1))
                nc.scalar.activation(kernel_high[:, slot, :], kernel_raw[:, slot, :], ACT.Copy
                                     ).then_inc(kernel_high_ready, 1)

            def table_high(k):
                act.wait_ge(lookup_loaded[k], 32)
                if k > 0:
                    act.wait_ge(field_transposed, arrival(ONE_HOT_FIELDS[k - 1]) + 1)
                nc.scalar.activation(table_parts[0:ONE_HOT_PARTS, :, 0:EMB],
                                     lookup_tables[k][0:ONE_HOT_PARTS], ACT.Copy
                                     ).then_inc(table_high_ready, 1)

            for step in range(STEPS):
                if step == 0:
                    kernel_group_high(0)
                    kernel_group_high(1)
                for event, field, part in field_events[step]:
                    if event == "prepare" and part == 0:
                        table_high(ONE_HOT_FIELDS.index(field))
                    if event != "take" or part == 0:
                        continue
                    n = arrival(field)
                    slot, half = n % MOVING_SLOTS, EMB * (field % 2)
                    act.wait_ge(field_transposed, n + 1)
                    if n >= MOVING_SLOTS and last_inner_of_field(n - MOVING_SLOTS):
                        act.wait_ge(inner_ready, last_inner_of_field(n - MOVING_SLOTS))
                    if field in ONE_HOT_FIELDS:
                        nc.scalar.activation(moving[:, slot, :], field_t[:, :], ACT.Copy
                                             ).then_inc(field_copied, 1)
                    else:
                        for odd in range(2):
                            nc.scalar.activation(by_tiles(moving[0:EMB, slot, :], odd), transposed_tiles(n, odd), ACT.Copy)
                        for odd in range(2):
                            last = nc.scalar.activation(by_tiles(fields[half:half + EMB, field // 2, :], odd),
                                                        transposed_tiles(n, odd), ACT.Copy)
                        last.then_inc(field_copied, 1)
                if step == HEAD_STEP:
                    act.wait_ge(head_weights_made, 1)
                    for q in range(UNITS_PER_STEP):
                        last = nc.scalar.activation(w_head[:, 2 * q:2 * q + 2, :], inner[q][:, :, :], ACT.Copy)
                    last.then_inc(head_weights_ready, 1)
                if group_made_at(step) is not None:
                    kernel_group_high(group_made_at(step))

            def relu_tiles(dst, banks, made, made_count, bias, ready, tiles, half):
                act.wait_ge(made, made_count)
                for t in range(tiles):
                    last = nc.scalar.activation(dst[:, t, HALF * half:HALF * (half + 1)], banks[t],
                                                ACT.Relu, bias=bias[:, t:t + 1])
                last.then_inc(ready, 1)

            act.wait_ge(head_bias_ready, 1)
            for half in range(HALVES):
                relu_tiles(h1, h1_banks(half), h1_made, half + 1, b_head, h1_ready, H1_TILES, half)
            for half in range(HALVES):
                relu_tiles(h2, h2_banks(half), h2_made, half + 1, b_top2_sb, h2_ready, H2_TILES, half)
            act.wait_ge(y_made, 1)
            for quarter in range(4):
                last = nc.scalar.activation(y_row[:, BATCH // 4 * quarter:BATCH // 4 * (quarter + 1)],
                                            y_part(quarter), ACT.Copy)
            last.then_inc(y_ready, 1)

        @block.vector
        def _(dve):
            def kernel_group_rest(group):
                slot = group % KERNEL_SLOTS
                dve.wait_ge(kernel_high_ready, group + 1)
                nc.vector.tensor_tensor(kernel_rest[:, slot, :], kernel_raw[:, slot, :],
                                        kernel_high[:, slot, :].bitcast(f32), ALU.subtract
                                        ).then_inc(kernel_rest_ready, 1)

            def add_sums(step):
                tile, half = step // HALVES // POSITIONS, step % HALVES
                cols = slice(HALF * half, HALF * (half + 1))
                dve.wait_ge(step_reduced, step + 1)
                nc.vector.tensor_tensor(sums[:, tile, cols], row_sums[:, half, :], sums[:, tile, cols],
                                        ALU.add).then_inc(sums_ready, 1)

            def split_table(field):
                k = ONE_HOT_FIELDS.index(field)
                dve.wait_ge(table_high_ready, k + 1)
                nc.vector.tensor_tensor(table_parts[0:ONE_HOT_PARTS, :, EMB:2 * EMB],
                                        lookup_tables[k][0:ONE_HOT_PARTS],
                                        table_parts[0:ONE_HOT_PARTS, :, 0:EMB].bitcast(f32), ALU.subtract
                                        ).then_inc(table_rest_ready, 1)

            def one_hot_tiles(field, first, last):
                k = ONE_HOT_FIELDS.index(field)
                dve.wait_ge(lookup_loaded[k], 32)
                for tile in range(first, last):
                    made = ONE_HOT_TILES * k + tile
                    if made >= ONE_HOT_SLOTS:
                        dve.wait_ge(one_hot_used, made + 1 - ONE_HOT_SLOTS)
                    nc.vector.tensor_scalar(one_hot[0:ONE_HOT_PARTS, made % ONE_HOT_SLOTS, :],
                                            lookup_ids[k][0:ONE_HOT_PARTS],
                                            one_hot_row_sb[0:ONE_HOT_PARTS, tile:tile + 1], None,
                                            ALU.is_equal).then_inc(one_hot_made, 1)

            def split_field(field, part):
                n = arrival(field)
                slot, half = n % MOVING_SLOTS, EMB * (field % 2)
                cols = slice(HALF * part, HALF * (part + 1))
                dve.wait_ge(field_copied, n + 1)
                if field in ONE_HOT_FIELDS:
                    nc.vector.tensor_tensor(fields[half:half + EMB, field // 2, cols], field_t[EMB:P, cols],
                                            moving[0:EMB, slot, cols].bitcast(f32), ALU.add
                                            ).then_inc(field_split, 1)
                else:
                    nc.vector.tensor_tensor(by_tiles(moving[EMB:P, slot, :], part), transposed_tiles(n, part),
                                            by_tiles(moving[0:EMB, slot, :].bitcast(f32), part), ALU.subtract
                                            ).then_inc(field_split, 1)

            nc.vector.memset(sums[:, :, :], 0.0).then_inc(sums_zeroed, 1)
            nc.vector.memset(selector[:, :], 0.0).then_inc(selector_zeroed, 1)
            dve.wait_ge(selector_zeroed, 1)
            nc.vector.memset(selector[0:EMB, 2 * POSITIONS - 2:2 * POSITIONS - 1], 1.0)
            nc.vector.memset(selector[EMB:P, 2 * POSITIONS - 1:2 * POSITIONS], 1.0).then_inc(selector_ready, 1)
            dve.wait_ge(lookup_rows_loaded, 16)
            for step in range(STEPS):
                for event, field, part in field_events[step]:
                    if event == "split":
                        split_field(field, part)
                    elif event == "prepare":
                        if part == 0:
                            split_table(field)
                        one_hot_tiles(field, ONE_HOT_SLOTS * part, ONE_HOT_SLOTS * (part + 1))
                if step == 0:
                    kernel_group_rest(0)
                    kernel_group_rest(1)
                if step == HEAD_STEP:
                    dve.wait_ge(head_bias_made, 1)
                    nc.vector.tensor_tensor(b_head[:, :], inner[0][:, 0, 0:H1_TILES], b_top1_sb[:, :], ALU.add
                                            ).then_inc(head_bias_ready, 1)
                    dve.wait_ge(dense_loaded, 16 * len(LONE_UNITS))
                half = step % HALVES
                cols = slice(HALF * half, HALF * (half + 1))
                for q in range(UNITS_PER_STEP):
                    unit = UNITS[unit_of(step, q)]
                    dst = products[:, step % PRODUCT_SLOTS, 2 * q:2 * q + 2, :]
                    dve.wait_ge(inner_ready, inner_count(step, q))
                    if q == 0 and step >= PRODUCT_SLOTS:
                        dve.wait_ge(step_reduced, step + 1 - PRODUCT_SLOTS)
                    there = max(arrival(2 * m + parity) for m in unit[2 if unit[0] == "full" else 1:]
                                for parity in range(2)) + 1
                    dve.wait_ge(field_copied, there)
                    dve.wait_ge(field_split, HALVES * there)
                    if unit[0] == "full":
                        second = fields[:, unit[2]:unit[2] + 1, cols].to_broadcast([P, 2, HALF])
                        nc.vector.tensor_tensor(dst, inner[q][:, :, :], second, ALU.mult
                                                ).then_inc(product_ready, 1)
                    else:
                        second = fields[EMB:P, unit[1]:unit[2] + 1:unit[2] - unit[1], cols]
                        nc.vector.tensor_tensor(dst[EMB:P], inner[q][EMB:P, :, :], second, ALU.mult
                                                ).then_inc(product_ready, 1)
                    if q == 0 and step >= 2 and closes_tile(step - 2):
                        add_sums(step - 2)
                group = group_made_at(step)
                if group is not None and group < FIRST_POOL_GROUP:
                    kernel_group_rest(group)
            add_sums(STEPS - 2)
            add_sums(STEPS - 1)

        @block.tensor
        def _(pe):
            matmul = nc.tensor.matmul

            def reduce(step):
                tile_step, half = step // HALVES, step % HALVES
                position = tile_step % POSITIONS
                columns = selector[:, 2 * (POSITIONS - 1 - position):][:, 0:2 * POSITIONS]
                if position == 0 and tile_step >= POSITIONS:
                    pe.wait_ge(sums_ready, HALVES * (tile_step // POSITIONS - 1) + half + 1)
                pe.wait_ge(product_ready, UNITS_PER_STEP * (step + 1))
                for q in range(UNITS_PER_STEP):
                    rows = slice(0, P) if UNITS[unit_of(step, q)][0] == "full" else slice(EMB, P)
                    for chunk in range(2):
                        s = 2 * q + chunk
                        last = matmul(row_sums[32 * s:32 * s + 32, half, :], columns[rows],
                                      products[rows, step % PRODUCT_SLOTS, s, :],
                                      start=position == 0, stop=position == POSITIONS - 1,
                                      tile_position=(rows.start, 32 * s))
                last.then_inc(step_reduced, 1)

            def make_head_weights():
                pe.wait_ge(weights_loaded, 16 * 9)
                if HEAD_STEP > 0:
                    pe.wait_ge(product_ready, UNITS_PER_STEP * HEAD_STEP)
                for t in range(H1_TILES):
                    for part in range(2):
                        last = matmul(inner[0][:, 0, t:t + 1], w_top1_sb[:, part, P * t:P * (t + 1)],
                                      b_rec_sb[:, part:part + 1], start=part == 0, stop=part == 1)
                last.then_inc(head_bias_made, 1)
                for tile in reversed(range(ROW_TILES)):
                    if tile == 0:
                        pe.wait_ge(head_bias_ready, 1)
                    for part, rows in ((0, P), (1, P), (2, DENSE)):
                        last = matmul(inner[tile // 2][:, tile % 2, :],
                                      w_rows_sb[0:rows, part, P * tile:P * (tile + 1)],
                                      w_top1_sb[0:rows, part, :], start=part == 0, stop=part == 2)
                last.then_inc(head_weights_made, 1)
                pe.wait_ge(head_weights_ready, 1)

            def take_field(field, part):
                n = arrival(field)
                if n > 0:
                    pe.wait_ge(field_split, HALVES * bank_holder(n))
                if field in ONE_HOT_FIELDS:
                    k = ONE_HOT_FIELDS.index(field)
                    pe.wait_ge(table_rest_ready, k + 1)
                    for tile in range(ONE_HOT_SLOTS * part, ONE_HOT_SLOTS * (part + 1)):
                        made = ONE_HOT_TILES * k + tile
                        pe.wait_ge(one_hot_made, made + 1)
                        for half in range(HALVES):
                            cols = slice(HALF * half, HALF * (half + 1))
                            last = matmul(field_t[:, cols], table_parts[0:ONE_HOT_PARTS, tile, :],
                                          one_hot[0:ONE_HOT_PARTS, made % ONE_HOT_SLOTS, cols],
                                          start=tile == 0, stop=tile == ONE_HOT_TILES - 1)
                        last.then_inc(one_hot_used, 1)
                    if part == 1:
                        pe.wait_ge(one_hot_used, ONE_HOT_TILES * (k + 1))
                        pe.sem_inc(field_transposed, 1)
                    return
                g = GATHERED_FIELDS.index(field)
                pe.wait_ge(field_gathered[g % GATHER_SLOTS], 16 * B_TILES * (g // GATHER_SLOTS + 1))
                for t in range(B_TILES // 2):
                    two_tiles = gathered[:, g % GATHER_SLOTS, 2 * t:2 * t + 2, :].rearrange("p t e -> p (t e)")
                    last = nc.tensor.transpose(transposed(n)[:, P * t:P * (t + 1)], two_tiles, identity_sb[:, :])
                last.then_inc(field_transposed, 1)

            pe.wait_ge(selector_ready, 1)
            pe.wait_ge(identity_loaded, 16)
            for step in range(STEPS):
                for event, field, part in field_events[step]:
                    if event == "take":
                        take_field(field, part)
                if step == HEAD_STEP:
                    make_head_weights()
                half = step % HALVES
                cols = slice(HALF * half, HALF * (half + 1))
                for q in range(UNITS_PER_STEP):
                    u = unit_of(step, q)
                    group = u // GROUP_UNITS
                    kslot = group % KERNEL_SLOTS
                    pe.wait_ge(kernel_rest_ready, group + 1)
                    pe.wait_ge(field_split, HALVES * (max(arrival(f) for f in unit_fields(UNITS[u])) + 1))
                    if step > 0:
                        pe.wait_ge(product_ready, UNITS_PER_STEP * (step - 1) + q + 1)
                    for chunk in range(2):
                        mslot = arrival(unit_fields(UNITS[u])[chunk]) % MOVING_SLOTS
                        at = (2 * (u % GROUP_UNITS) + chunk) * P
                        for part, kernel_part in enumerate((kernel_high, kernel_rest)):
                            last = matmul(inner[q][:, chunk, :], kernel_part[:, kslot, at:at + P],
                                          moving[:, mslot, cols], start=part == 0, stop=part == 1)
                    last.then_inc(inner_ready, 1)
                if step > 0:
                    reduce(step - 1)
            reduce(STEPS - 1)

            pe.wait_ge(weights_loaded, 16 * 9)
            pe.wait_ge(product_ready, UNITS_PER_STEP * STEPS)
            for half in range(HALVES):
                cols = slice(HALF * half, HALF * (half + 1))
                for tile in range(ROW_TILES):
                    if half == 1 or tile == ROW_TILES - 1:
                        pe.wait_ge(sums_ready, HALVES * (ROW_TILES - 1) + (HALVES if half else 1))
                    for t in range(H1_TILES):
                        last = matmul(h1_banks(half)[t], w_head[:, tile, P * t:P * (t + 1)],
                                      sums[:, tile, cols], start=tile == 0, stop=tile == ROW_TILES - 1)
                last.then_inc(h1_made, 1)
            for half in range(HALVES):
                cols = slice(HALF * half, HALF * (half + 1))
                pe.wait_ge(h1_ready, half + 1)
                for t in range(H2_TILES):
                    for part in range(H1_TILES):
                        last = matmul(h2_banks(half)[t], w_top2_sb[:, part, P * t:P * (t + 1)],
                                      h1[:, part, cols], start=part == 0, stop=part == H1_TILES - 1)
                last.then_inc(h2_made, 1)
            pe.wait_ge(h2_ready, HALVES)
            for part in range(H2_TILES):
                for quarter in range(4):
                    cols = slice(BATCH // 4 * quarter, BATCH // 4 * (quarter + 1))
                    last = matmul(y_part(quarter), w_top3_sb[:, part:part + 1], h2[:, part, cols],
                                  start=part == 0, stop=part == H2_TILES - 1,
                                  tile_position=(0, 32 * quarter))
            last.then_inc(y_made, 1)


def lay_out(inputs):
    import numpy as np

    arrays = {}
    ids = np.asarray(inputs["ids"])
    arrays["ids"] = np.ascontiguousarray(
        ids.reshape(B_TILES, P, FIELDS).transpose(1, 0, 2).reshape(P, B_TILES * FIELDS))
    arrays["ids_t"] = np.ascontiguousarray(ids.T)
    arrays["one_hot_row"] = np.arange(ONE_HOT_ROWS, dtype=np.float32).reshape(ONE_HOT_PARTS, ONE_HOT_TILES)
    for f in range(FIELDS):
        arrays[f"tbl_{f}"] = np.ascontiguousarray(inputs[f"tbl_{f}"])
    by_pair = np.asarray(inputs["L0_rec_kernel"]).transpose(1, 2, 0)
    w = np.asarray(inputs["L0_rec_W"])
    stream = np.empty((len(UNITS), 2, 2, EMB, EMB), by_pair.dtype)
    w_rows = np.zeros((Z_DIM + DENSE, ROWS), w.dtype)
    for u, unit in enumerate(UNITS):
        for chunk, field in enumerate(unit_fields(unit)):
            for parity in range(2):
                second = 2 * unit[2] + parity if unit[0] == "full" else field + 1
                p = pair_index(field, second)
                stream[u, chunk, parity] = by_pair[p] if field < second else by_pair[p].T
                if unit[0] == "full" or parity == 1:
                    w_rows[:Z_DIM, row_of(u, chunk, parity)] = w[:, p]
    for k, u in enumerate(LONE_UNITS):
        for chunk in range(2):
            w_rows[Z_DIM + 2 * k + chunk, row_of(u, chunk, 0)] = 1
    arrays["kernel_stream"] = np.ascontiguousarray(
        stream.reshape(GROUPS, GROUP_UNITS * 4, EMB, EMB).transpose(0, 2, 1, 3).reshape(GROUPS, EMB, GROUP_COLS))
    arrays["w_rows"] = w_rows
    arrays["w_top1"] = np.ascontiguousarray(inputs["W_top1"])
    arrays["b_rec"] = np.ascontiguousarray(np.asarray(inputs["L0_rec_b"]).reshape(-1, P).T)
    arrays["b_top1"] = np.ascontiguousarray(np.asarray(inputs["b_top1"]).reshape(-1, P).T)
    arrays["w_top2"] = np.ascontiguousarray(inputs["W_top2"])
    arrays["b_top2"] = np.ascontiguousarray(np.asarray(inputs["b_top2"]).reshape(-1, P).T)
    arrays["w_top3"] = np.ascontiguousarray(np.asarray(inputs["W_top3"]).reshape(-1, P).T)
    arrays["dense_t"] = np.ascontiguousarray(np.asarray(inputs["dense_ctx"]).T)
    arrays["identity"] = np.eye(P, dtype=np.float32)
    return arrays


def kernel(**inputs):
    import numpy as np
    import concourse.bacc as bacc
    from concourse.bass_utils import run_bass_kernel_spmd

    nc = bacc.Bacc("TRN2", target_bir_lowering=False, num_devices=1)
    arrays, aps = {}, {}
    for name, a in lay_out(inputs).items():
        arrays[f"in_{name}"] = a
        aps[name] = nc.dram_tensor(f"in_{name}", a.shape, mybir.dt.from_np(a.dtype), kind="ExternalInput").ap()
    out = nc.dram_tensor("out_y", (BATCH, 1), mybir.dt.float32, kind="ExternalOutput").ap()
    tables = [aps.pop(f"tbl_{f}") for f in range(FIELDS)]
    dlrm_tower(nc, aps.pop("ids"), tables=tables, out=out, **aps)
    return run_bass_kernel_spmd(nc, [arrays], core_ids=[0]).results[0]["out_y"]
```

```python
import concourse.bass as bass
from concourse import mybir
from contextlib import ExitStack

EMB = 64
FIELDS = 32
BATCH = 1024
P = 128
HALF = 512
HALVES = BATCH // HALF
B_TILES = BATCH // P
FPAIRS = FIELDS // 2
DENSE = 16
Z_DIM, H1_DIM, H2_DIM = 256, 512, 256
H1_TILES, H2_TILES = H1_DIM // P, H2_DIM // P

PAIR_ORDER = (15, 14, 13, 10, 9, 7, 12, 11, 8, 6, 5, 4, 3, 2, 1, 0)
ONE_HOT_FIELDS = (31, 29, 27, 21, 18)
ONE_HOT_ROWS = 1000
ONE_HOT_TILES = 8
ONE_HOT_PARTS = ONE_HOT_ROWS // ONE_HOT_TILES
ONE_HOT_SLOTS = 4
TABLE_SLOTS = 3
FIELD_ORDER = [f for m in PAIR_ORDER
               for f in sorted((2 * m, 2 * m + 1), key=lambda f: f not in ONE_HOT_FIELDS)]
GATHERED_FIELDS = [f for f in FIELD_ORDER if f not in ONE_HOT_FIELDS]

UNITS = []
for _at, _m in enumerate(PAIR_ORDER):
    UNITS += [("full", _m, _n) for _n in PAIR_ORDER[:_at]]
    if _at % 2 == 1:
        UNITS.append(("lone", *sorted(PAIR_ORDER[_at - 1:_at + 1])))
UNITS_PER_STEP = 2
PAIR_STEPS = len(UNITS) // UNITS_PER_STEP
STEPS = PAIR_STEPS * HALVES
POSITIONS = 16
ROW_TILES = PAIR_STEPS // POSITIONS
ROWS = ROW_TILES * P
GROUP_UNITS = 4
GROUPS = len(UNITS) // GROUP_UNITS
GROUP_STEPS = GROUP_UNITS // UNITS_PER_STEP * HALVES
GROUP_COLS = GROUP_UNITS * 2 * P
KERNEL_SLOTS = 3
MOVING_SLOTS = 6
OPENING_FIELDS = 7
OPENING_LOOKUPS = sum(f in ONE_HOT_FIELDS for f in FIELD_ORDER[:OPENING_FIELDS])
MIDDLE_PAIRS = 8
GATHER_SLOTS = 4
PRODUCT_SLOTS = 2
SPLIT_PARTS = 4
FIRST_POOL_GROUP = 6


def unit_fields(unit):
    if unit[0] == "full":
        return 2 * unit[1] + 1, 2 * unit[1]
    return 2 * unit[1], 2 * unit[2]


def arrival(field):
    return FIELD_ORDER.index(field)


def unit_row(u, chunk, parity):
    step = u // UNITS_PER_STEP
    group = 2 * (u % UNITS_PER_STEP) + chunk
    return step // POSITIONS, 32 * group + 2 * (step % POSITIONS) + parity


def row_of(u, chunk, parity):
    tile, row = unit_row(u, chunk, parity)
    return tile * P + row


def pair_index(i, j):
    i, j = min(i, j), max(i, j)
    return i * FIELDS - i * (i + 1) // 2 + (j - i - 1)


LONE_UNITS = [u for u, unit in enumerate(UNITS) if unit[0] == "lone"]


def first_step(m):
    return min(u for u, unit in enumerate(UNITS) if m in unit[1:]) // UNITS_PER_STEP * HALVES


def steps_done_with(n):
    return 1 + max((u // UNITS_PER_STEP * HALVES + HALVES - 1 for u, unit in enumerate(UNITS)
                    if FIELD_ORDER[n] in unit_fields(unit)), default=-1)


LOOKUP_AHEAD = ((4, "prepare 0"), (3, "look up 0"), (3, "prepare 1"), (2, "look up 1"),
                (2, "split 01"), (2, "split 23"), (1, "take"), (0, "split 01"), (0, "split 23"))
FIRST_AHEAD = ((3, "take"), (2, "split 01"), (2, "split 23"))
MIDDLE_AHEAD = ((7, "take"), (5, "split 01"), (4, "split 23"), (3, "take"), (2, "split 01"), (1, "split 23"))
LATE_AHEAD = ((11, "take"), (9, "split 0"), (8, "split 1"), (7, "split 2"), (6, "split 3"),
              (6, "take"), (4, "split 0"), (3, "split 1"), (2, "split 2"), (1, "split 3"))
COPY_STEPS = 2


def field_plan():
    events = [[] for _ in range(STEPS)]
    step = 0
    for at in range(OPENING_FIELDS // 2, FPAIRS):
        arriving = FIELD_ORDER[2 * at:2 * at + 2]
        if 2 * at < OPENING_FIELDS:
            plan, second_at = FIRST_AHEAD, 0
        else:
            looked_up = arriving[0] in ONE_HOT_FIELDS
            plan = LOOKUP_AHEAD if looked_up else MIDDLE_AHEAD if at < MIDDLE_PAIRS else LATE_AHEAD
            second_at = [name for _, name in plan].index("take", 1)
        for place, (ahead, name) in enumerate(plan):
            step = max(step, first_step(PAIR_ORDER[at]) - ahead)
            if name == "take" and plan is LATE_AHEAD:
                step = max(step, steps_done_with(2 * at + (place >= second_at) - MOVING_SLOTS))
            if name == "split 0":
                step = max(step, taken + COPY_STEPS)
            if name == "take":
                taken = step
            event = name.rstrip(" 0123")
            parts = tuple(int(c) for c in name[len(event):].strip())
            events[step].append((event, arriving[place >= second_at], parts))
    return events


def dlrm_tower(nc, ids, ids_t, one_hot_row, tables, kernel_stream, w_rows, w_top1, b_rec, b_top1,
               w_top2, b_top2, w_top3, dense_t, identity, out):
    f32, f32r, i32 = mybir.dt.float32, mybir.dt.float32r, mybir.dt.int32
    ALU = mybir.AluOpType
    ACT = mybir.ActivationFunctionType
    field_events = field_plan()

    with ExitStack() as ctx:
        def sb(name, shape, dt=f32):
            return ctx.enter_context(nc.sbuf_tensor(name, shape, dt))

        def pb(name, shape):
            return ctx.enter_context(nc.psum_tensor(name, shape, f32))

        def sem(name):
            return ctx.enter_context(nc.semaphore(name))

        ids_sb = sb("ids_sb", [P, B_TILES * FIELDS], i32)
        gathered = sb("gathered", [P, GATHER_SLOTS, B_TILES, EMB])
        fields = sb("fields", [P, FPAIRS, BATCH])
        moving = sb("moving", [P, MOVING_SLOTS, BATCH], f32r)
        kernel_raw = sb("kernel_raw", [P, KERNEL_SLOTS, GROUP_COLS])
        kernel_high = sb("kernel_high", [P, KERNEL_SLOTS, GROUP_COLS], f32r)
        kernel_rest = sb("kernel_rest", [P, KERNEL_SLOTS, GROUP_COLS], f32r)
        products = sb("products", [P, PRODUCT_SLOTS, 2 * UNITS_PER_STEP, HALF])
        sums = sb("sums", [P, ROW_TILES, BATCH])
        w_head = sb("w_head", [P, ROW_TILES, H1_DIM])
        w_top2_sb = sb("w_top2_sb", [P, H1_TILES, H2_DIM])
        w_top3_sb = sb("w_top3_sb", [P, H2_TILES])
        b_rec_sb = sb("b_rec_sb", [P, Z_DIM // P])
        b_top1_sb = sb("b_top1_sb", [P, H1_TILES])
        b_head = sb("b_head", [P, H1_TILES])
        b_top2_sb = sb("b_top2_sb", [P, H2_TILES])
        identity_sb = sb("identity_sb", [P, P])
        one_hot_row_sb = sb("one_hot_row_sb", [P, ONE_HOT_TILES])
        one_hot = sb("one_hot", [P, ONE_HOT_SLOTS, BATCH], f32r)
        table_parts = sb("table_parts", [P, TABLE_SLOTS, ONE_HOT_TILES, 2 * EMB], f32r)
        selector = sb("selector", [P, 2 * (2 * POSITIONS) - 2])
        w_rows_sb = fields[:, 0, :].rearrange("p (t c) -> p t c", c=ROWS)
        w_top1_sb = fields[:, 1, :].rearrange("p (t c) -> p t c", c=H1_DIM)
        lookup_ids = [fields[:, m, :].bitcast(i32) for m in (3, 4, 5, 12, 2)]
        lookup_tables = [fields[:, m, HALF * part:HALF * (part + 1)].rearrange("p (k e) -> p k e", e=EMB)
                         for m, part in ((6, 0), (6, 1), (8, 0), (8, 1), (11, 0))]
        h1 = fields[:, 0:H1_TILES, :]
        h2 = fields[:, H1_TILES:H1_TILES + H2_TILES, :]
        y_row = fields[0:1, H1_TILES + H2_TILES, :]

        inner = [pb(f"inner{i}", [P, 2, HALF]) for i in range(UNITS_PER_STEP)]
        field_t = pb("field_t", [P, BATCH])
        row_sums = pb("row_sums", [P, HALVES, HALF])

        ids_loaded = sem("ids_loaded")
        identity_loaded = sem("identity_loaded")
        head_inputs_loaded = sem("head_inputs_loaded")
        weights_loaded = sem("weights_loaded")
        dense_loaded = sem("dense_loaded")
        sums_zeroed = sem("sums_zeroed")
        selector_zeroed = sem("selector_zeroed")
        selector_ready = sem("selector_ready")
        kernel_loaded = [sem(f"kernel_loaded{i}") for i in range(KERNEL_SLOTS)]
        kernel_high_ready = sem("kernel_high_ready")
        kernel_rest_ready = sem("kernel_rest_ready")
        field_gathered = [sem(f"field_gathered{i}") for i in range(GATHER_SLOTS)]
        lookup_rows_loaded = sem("lookup_rows_loaded")
        lookup_loaded = [sem(f"lookup_loaded{f}") for f in ONE_HOT_FIELDS]
        table_high_ready = sem("table_high_ready")
        table_rest_ready = sem("table_rest_ready")
        one_hot_made = sem("one_hot_made")
        one_hot_used = sem("one_hot_used")
        field_transposed = sem("field_transposed")
        field_copied = sem("field_copied")
        field_split = sem("field_split")
        inner_ready = sem("inner_ready")
        product_ready = sem("product_ready")
        step_reduced = sem("step_reduced")
        sums_ready = sem("sums_ready")
        head_weights_made = sem("head_weights_made")
        head_weights_ready = sem("head_weights_ready")
        head_bias_made = sem("head_bias_made")
        head_bias_ready = sem("head_bias_ready")
        h1_made = sem("h1_made")
        h1_ready = sem("h1_ready")
        h2_made = sem("h2_made")
        h2_ready = sem("h2_ready")
        y_made = sem("y_made")
        y_ready = sem("y_ready")
        y_stored = sem("y_stored")

        def inner_count(step, q):
            return UNITS_PER_STEP * step + q + 1

        def last_inner_of_field(n):
            users = [u for u, unit in enumerate(UNITS) if FIELD_ORDER[n] in unit_fields(unit)]
            if not users:
                return 0
            u = users[-1]
            return inner_count(u // UNITS_PER_STEP * HALVES + HALVES - 1, u % UNITS_PER_STEP)

        def closes_tile(step):
            return (step // HALVES) % POSITIONS == POSITIONS - 1

        def group_made_at(step):
            if step in (0, 2):
                return 1 + step // 2
            group = step // GROUP_STEPS + KERNEL_SLOTS - 1
            return group if step % GROUP_STEPS == 1 and KERNEL_SLOTS <= group < GROUPS else None

        def unit_of(step, q):
            return UNITS_PER_STEP * (step // HALVES) + q

        def by_tiles(row, odd):
            return row.rearrange("p (t odd b) -> p odd t b", odd=2, b=P)[:, odd, :, :]

        def transposed(field):
            bank = GATHERED_FIELDS.index(field) % 2
            return field_t[:, HALF * bank:HALF * (bank + 1)]

        def transposed_tiles(field, odd):
            return transposed(field)[EMB * odd:EMB * (odd + 1), :].rearrange("p (t b) -> p t b", b=P)

        def looked_up(k):
            if k >= OPENING_LOOKUPS:
                return field_t[:, :]
            return inner[k % UNITS_PER_STEP].rearrange("p a b -> p (a b)")

        def h1_banks(half):
            if half == 0:
                return [inner[0][:, 0, :], inner[0][:, 1, :], inner[1][:, 0, :], inner[1][:, 1, :]]
            return [field_t[:, 0:HALF], field_t[:, HALF:BATCH], row_sums[:, 0, :], row_sums[:, 1, :]]

        def h2_banks(half):
            return [inner[half][:, 0, :], inner[half][:, 1, :]]

        def y_part(quarter):
            return field_t[32 * quarter:32 * quarter + 1, 0:BATCH // 4]

        block = ctx.enter_context(nc.Block())

        @block.sync
        def _(sp):
            def load_group(slot, group):
                for part in range(2):
                    sp.dma_start(kernel_raw[EMB * part:EMB * (part + 1), slot, :],
                                 kernel_stream[group, :, :]).then_inc(kernel_loaded[slot], 16)

            def load_group_at(slot, group):
                for part in range(2):
                    sp.dma_start(kernel_raw[EMB * part:EMB * (part + 1), slot, :],
                                 kernel_stream[bass.ds(group, 1), :, :].rearrange("g e c -> (g e) c")
                                 ).then_inc(kernel_loaded[slot], 16)

            def load_lookup(k):
                field = ONE_HOT_FIELDS[k]
                sp.dma_start(lookup_ids[k], ids_t[field:field + 1, :].to_broadcast([P, BATCH])
                             ).then_inc(lookup_loaded[k], 16)
                sp.dma_start(lookup_tables[k][0:ONE_HOT_PARTS],
                             tables[field].rearrange("(p k) e -> p k e", k=ONE_HOT_TILES)
                             ).then_inc(lookup_loaded[k], 16)

            def load_head_input(src, dst):
                sp.dma_start(dst, src[0:Z_DIM, :].rearrange("(t p) c -> p t c", p=P)
                             ).then_inc(head_inputs_loaded, 16)

            sp.dma_start(ids_sb[:, :], ids).then_inc(ids_loaded, 16)
            sp.dma_start(one_hot_row_sb[0:ONE_HOT_PARTS, :], one_hot_row).then_inc(lookup_rows_loaded, 16)
            load_lookup(0)
            load_lookup(1)
            sp.dma_start(identity_sb[:, :], identity).then_inc(identity_loaded, 16)
            sp.dma_start(b_rec_sb[:, :], b_rec).then_inc(head_inputs_loaded, 16)
            sp.dma_start(b_top1_sb[:, :], b_top1).then_inc(head_inputs_loaded, 16)
            load_lookup(2)
            load_head_input(w_top1, w_top1_sb)
            load_head_input(w_rows, w_rows_sb)
            load_group(0, 0)
            load_group(1, 1)
            load_group(2, 2)
            for k in range(3, len(ONE_HOT_FIELDS)):
                load_lookup(k)
            sp.wait_ge(sums_zeroed, 1)
            for k, u in enumerate(LONE_UNITS):
                tile, row = unit_row(u, 0, 0)
                sp.dma_start(sums[row:row + 33:32, tile, :], dense_t[2 * k:2 * k + 2, :]
                             ).then_inc(dense_loaded, 16)
            sp.dma_start(b_top2_sb[:, :], b_top2).then_inc(weights_loaded, 16)
            sp.dma_start(w_top3_sb[:, :], w_top3).then_inc(weights_loaded, 16)
            sp.dma_start(w_top2_sb[:, :, :], w_top2.rearrange("(t p) c -> p t c", p=P)
                         ).then_inc(weights_loaded, 16)
            sp.wait_ge(head_weights_ready, ROW_TILES)
            for k, u in enumerate(LONE_UNITS):
                tile, row = unit_row(u, 0, 0)
                sp.dma_start(w_head[row:row + 33:32, tile, :], w_top1[Z_DIM + 2 * k:Z_DIM + 2 * k + 2, :]
                             ).then_inc(weights_loaded, 16)
            looped = (GROUPS - KERNEL_SLOTS) // KERNEL_SLOTS * KERNEL_SLOTS
            with sp.Fori(KERNEL_SLOTS, KERNEL_SLOTS + looped, KERNEL_SLOTS) as group:
                for slot in range(KERNEL_SLOTS):
                    sp.wait_ge(kernel_rest_ready, group + (slot + 1 - KERNEL_SLOTS))
                    load_group_at(slot, group + slot)
            for group in range(KERNEL_SLOTS + looped, GROUPS):
                sp.wait_ge(kernel_rest_ready, group + 1 - KERNEL_SLOTS)
                load_group(group % KERNEL_SLOTS, group)
            sp.wait_ge(y_ready, 1)
            sp.dma_start(out.rearrange("b o -> o b"), y_row).then_inc(y_stored, 16)
            sp.wait_ge(y_stored, 16)

        @block.gpsimd
        def _(pool):
            def gather_field(n):
                field = GATHERED_FIELDS[n]
                slot = n % GATHER_SLOTS
                if n >= GATHER_SLOTS:
                    pool.wait_ge(field_transposed, n - GATHER_SLOTS + 1)
                for t in range(B_TILES):
                    column = t * FIELDS + field
                    nc.gpsimd.indirect_dma_start(
                        gathered[:, slot, t, :], None, tables[field],
                        bass.IndirectOffsetOnAxis(ap=ids_sb[:, column:column + 1], axis=0),
                    ).then_inc(field_gathered[slot], 16)

            def kernel_group_rest(group):
                slot = group % KERNEL_SLOTS
                pool.wait_ge(kernel_high_ready, group + 1)
                nc.gpsimd.tensor_tensor(kernel_rest[:, slot, :], kernel_raw[:, slot, :],
                                        kernel_high[:, slot, :].bitcast(f32), ALU.subtract
                                        ).then_inc(kernel_rest_ready, 1)

            pool.wait_ge(ids_loaded, 16)
            n, taken = 0, sum(f in GATHERED_FIELDS for f in FIELD_ORDER[:OPENING_FIELDS])
            for step in range(STEPS):
                taken += sum(e[0] == "take" and e[1] in GATHERED_FIELDS for e in field_events[step])
                while n < min(taken + GATHER_SLOTS, len(GATHERED_FIELDS)):
                    gather_field(n)
                    n += 1
                group = group_made_at(step)
                if group is not None and group >= FIRST_POOL_GROUP:
                    if group == FIRST_POOL_GROUP:
                        pool.wait_ge(kernel_rest_ready, FIRST_POOL_GROUP)
                    kernel_group_rest(group)

        @block.scalar
        def _(act):
            def kernel_group_high(group):
                slot = group % KERNEL_SLOTS
                act.wait_ge(kernel_loaded[slot], 32 * (group // KERNEL_SLOTS + 1))
                if group >= KERNEL_SLOTS:
                    act.wait_ge(inner_ready, inner_count(GROUP_STEPS * (group + 1 - KERNEL_SLOTS) - 1,
                                                         UNITS_PER_STEP - 1))
                nc.scalar.activation(kernel_high[:, slot, :], kernel_raw[:, slot, :], ACT.Copy
                                     ).then_inc(kernel_high_ready, 1)

            def table_high(k):
                act.wait_ge(lookup_loaded[k], 32)
                if k >= TABLE_SLOTS:
                    act.wait_ge(one_hot_used, ONE_HOT_TILES * (k - TABLE_SLOTS + 1))
                nc.scalar.activation(table_parts[0:ONE_HOT_PARTS, k % TABLE_SLOTS, :, 0:EMB],
                                     lookup_tables[k][0:ONE_HOT_PARTS], ACT.Copy
                                     ).then_inc(table_high_ready, 1)

            def copy_field(field):
                n = arrival(field)
                slot, half = n % MOVING_SLOTS, EMB * (field % 2)
                if n >= MOVING_SLOTS:
                    act.wait_ge(field_split, SPLIT_PARTS * (n - MOVING_SLOTS + 1))
                    if last_inner_of_field(n - MOVING_SLOTS):
                        act.wait_ge(inner_ready, last_inner_of_field(n - MOVING_SLOTS))
                if field in ONE_HOT_FIELDS:
                    k = ONE_HOT_FIELDS.index(field)
                    act.wait_ge(one_hot_used, ONE_HOT_TILES * (k + 1))
                    nc.scalar.activation(moving[:, slot, :], looked_up(k), ACT.Copy).then_inc(field_copied, 1)
                else:
                    act.wait_ge(field_transposed, GATHERED_FIELDS.index(field) + 1)
                    for odd in range(2):
                        nc.scalar.activation(by_tiles(moving[0:EMB, slot, :], odd),
                                             transposed_tiles(field, odd), ACT.Copy)
                    for odd in range(2):
                        last = nc.scalar.activation(by_tiles(fields[half:half + EMB, field // 2, :], odd),
                                                    transposed_tiles(field, odd), ACT.Copy)
                    last.then_inc(field_copied, 1)

            def copy_head_weights(tile, made):
                act.wait_ge(head_weights_made, made)
                nc.scalar.activation(w_head[:, tile, :], row_sums[:, tile % 2, :], ACT.Copy
                                     ).then_inc(head_weights_ready, 1)

            table_high(0)
            table_high(1)
            copy_field(FIELD_ORDER[0])
            table_high(2)
            copy_field(FIELD_ORDER[1])
            copy_field(FIELD_ORDER[2])
            kernel_group_high(0)
            copy_head_weights(3, 1)
            table_high(3)
            copy_head_weights(2, 2)
            copy_field(FIELD_ORDER[3])
            copy_field(FIELD_ORDER[4])
            copy_head_weights(1, 3)
            copy_field(FIELD_ORDER[5])
            copy_field(FIELD_ORDER[6])
            copy_head_weights(0, 4)

            for step in range(STEPS):
                for event, field, parts in field_events[step]:
                    if event == "prepare" and parts == (0,):
                        table_high(ONE_HOT_FIELDS.index(field))
                    if event == "take" or (event == "look up" and parts == (1,)):
                        copy_field(field)
                if group_made_at(step) is not None:
                    kernel_group_high(group_made_at(step))

            def relu_tiles(dst, banks, made, made_count, bias, ready, tiles, half):
                act.wait_ge(made, made_count)
                for t in range(tiles):
                    last = nc.scalar.activation(dst[:, t, HALF * half:HALF * (half + 1)], banks[t],
                                                ACT.Relu, bias=bias[:, t:t + 1])
                last.then_inc(ready, 1)

            act.wait_ge(head_bias_ready, 1)
            for half in range(HALVES):
                relu_tiles(h1, h1_banks(half), h1_made, half + 1, b_head, h1_ready, H1_TILES, half)
            for half in range(HALVES):
                relu_tiles(h2, h2_banks(half), h2_made, half + 1, b_top2_sb, h2_ready, H2_TILES, half)
            act.wait_ge(y_made, 1)
            for quarter in range(4):
                last = nc.scalar.activation(y_row[:, BATCH // 4 * quarter:BATCH // 4 * (quarter + 1)],
                                            y_part(quarter), ACT.Copy)
            last.then_inc(y_ready, 1)

        @block.vector
        def _(dve):
            def kernel_group_rest(group):
                slot = group % KERNEL_SLOTS
                dve.wait_ge(kernel_high_ready, group + 1)
                nc.vector.tensor_tensor(kernel_rest[:, slot, :], kernel_raw[:, slot, :],
                                        kernel_high[:, slot, :].bitcast(f32), ALU.subtract
                                        ).then_inc(kernel_rest_ready, 1)

            def add_sums(step):
                tile, half = step // HALVES // POSITIONS, step % HALVES
                cols = slice(HALF * half, HALF * (half + 1))
                dve.wait_ge(step_reduced, step + 1)
                nc.vector.tensor_tensor(sums[:, tile, cols], row_sums[:, half, :], sums[:, tile, cols],
                                        ALU.add).then_inc(sums_ready, 1)

            def table_rest(k):
                dve.wait_ge(table_high_ready, k + 1)
                nc.vector.tensor_tensor(table_parts[0:ONE_HOT_PARTS, k % TABLE_SLOTS, :, EMB:2 * EMB],
                                        lookup_tables[k][0:ONE_HOT_PARTS],
                                        table_parts[0:ONE_HOT_PARTS, k % TABLE_SLOTS, :, 0:EMB].bitcast(f32),
                                        ALU.subtract
                                        ).then_inc(table_rest_ready, 1)

            def one_hot_tiles(k, first, last):
                dve.wait_ge(lookup_loaded[k], 32)
                for tile in range(first, last):
                    made = ONE_HOT_TILES * k + tile
                    if made >= ONE_HOT_SLOTS:
                        dve.wait_ge(one_hot_used, made + 1 - ONE_HOT_SLOTS)
                    nc.vector.tensor_scalar(one_hot[0:ONE_HOT_PARTS, made % ONE_HOT_SLOTS, :],
                                            lookup_ids[k][0:ONE_HOT_PARTS],
                                            one_hot_row_sb[0:ONE_HOT_PARTS, tile:tile + 1], None,
                                            ALU.is_equal).then_inc(one_hot_made, 1)

            def split_field(field, parts):
                n = arrival(field)
                slot, half = n % MOVING_SLOTS, EMB * (field % 2)
                dve.wait_ge(field_copied, n + 1)
                if field in ONE_HOT_FIELDS:
                    cols = slice(BATCH // SPLIT_PARTS * parts[0], BATCH // SPLIT_PARTS * (parts[-1] + 1))
                    nc.vector.tensor_tensor(fields[half:half + EMB, field // 2, cols],
                                            looked_up(ONE_HOT_FIELDS.index(field))[EMB:P, cols],
                                            moving[0:EMB, slot, cols].bitcast(f32), ALU.add
                                            ).then_inc(field_split, len(parts))
                else:
                    odd, tiles = parts[0] // 2, slice(2 * (parts[0] % 2), 2 * (parts[-1] % 2) + 2)
                    nc.vector.tensor_tensor(by_tiles(moving[EMB:P, slot, :], odd)[:, tiles, :],
                                            transposed_tiles(field, odd)[:, tiles, :],
                                            by_tiles(moving[0:EMB, slot, :].bitcast(f32), odd)[:, tiles, :],
                                            ALU.subtract).then_inc(field_split, len(parts))

            def split_whole_field(n):
                for parts in ((0, 1), (2, 3)):
                    split_field(FIELD_ORDER[n], parts)

            nc.vector.memset(selector[:, :], 0.0).then_inc(selector_zeroed, 1)
            nc.vector.memset(sums[:, :, :], 0.0).then_inc(sums_zeroed, 1)
            dve.wait_ge(selector_zeroed, 1)
            nc.vector.memset(selector[0:EMB, 2 * POSITIONS - 2:2 * POSITIONS - 1], 1.0)
            nc.vector.memset(selector[EMB:P, 2 * POSITIONS - 1:2 * POSITIONS], 1.0).then_inc(selector_ready, 1)
            dve.wait_ge(lookup_rows_loaded, 16)
            one_hot_tiles(0, 0, 2)
            table_rest(0)
            one_hot_tiles(0, 2, 8)
            table_rest(1)
            one_hot_tiles(1, 0, 4)
            split_whole_field(0)
            one_hot_tiles(1, 4, 8)
            table_rest(2)
            one_hot_tiles(2, 0, 4)
            split_whole_field(1)
            dve.wait_ge(head_bias_made, 1)
            nc.vector.tensor_tensor(b_head[:, :], row_sums[:, 0, 0:H1_TILES], b_top1_sb[:, :], ALU.add
                                    ).then_inc(head_bias_ready, 1)
            split_whole_field(2)
            kernel_group_rest(0)
            one_hot_tiles(2, 4, 8)
            table_rest(3)
            one_hot_tiles(3, 0, 4)
            split_whole_field(3)
            one_hot_tiles(3, 4, 8)
            split_whole_field(4)
            split_whole_field(5)
            split_whole_field(6)

            for step in range(STEPS):
                for event, field, parts in field_events[step]:
                    if event == "prepare":
                        if parts == (0,):
                            table_rest(ONE_HOT_FIELDS.index(field))
                        one_hot_tiles(ONE_HOT_FIELDS.index(field), 4 * parts[0], 4 * parts[0] + 4)
                    if event == "split":
                        split_field(field, parts)
                half = step % HALVES
                cols = slice(HALF * half, HALF * (half + 1))
                for q in range(UNITS_PER_STEP):
                    unit = UNITS[unit_of(step, q)]
                    dst = products[:, step % PRODUCT_SLOTS, 2 * q:2 * q + 2, :]
                    dve.wait_ge(inner_ready, inner_count(step, q))
                    if q == 0 and step >= PRODUCT_SLOTS:
                        dve.wait_ge(step_reduced, step + 1 - PRODUCT_SLOTS)
                    there = max(arrival(2 * m + parity) for m in unit[2 if unit[0] == "full" else 1:]
                                for parity in range(2)) + 1
                    dve.wait_ge(field_copied, there)
                    dve.wait_ge(field_split, SPLIT_PARTS * there)
                    if unit[0] == "full":
                        second = fields[:, unit[2]:unit[2] + 1, cols].to_broadcast([P, 2, HALF])
                        nc.vector.tensor_tensor(dst, inner[q][:, :, :], second, ALU.mult
                                                ).then_inc(product_ready, 1)
                    else:
                        second = fields[EMB:P, unit[1]:unit[2] + 1:unit[2] - unit[1], cols]
                        nc.vector.tensor_tensor(dst[EMB:P], inner[q][EMB:P, :, :], second, ALU.mult
                                                ).then_inc(product_ready, 1)
                    if q == 0 and step >= 2 and closes_tile(step - 2):
                        if step - 2 < HALVES * POSITIONS:
                            dve.wait_ge(dense_loaded, 16 * len(LONE_UNITS))
                        add_sums(step - 2)
                group = group_made_at(step)
                if group is not None and group < FIRST_POOL_GROUP:
                    kernel_group_rest(group)
            add_sums(STEPS - 2)
            add_sums(STEPS - 1)

        @block.tensor
        def _(pe):
            matmul = nc.tensor.matmul

            def reduce(step):
                tile_step, half = step // HALVES, step % HALVES
                position = tile_step % POSITIONS
                columns = selector[:, 2 * (POSITIONS - 1 - position):][:, 0:2 * POSITIONS]
                if position == 0 and tile_step >= POSITIONS:
                    pe.wait_ge(sums_ready, HALVES * (tile_step // POSITIONS - 1) + half + 1)
                pe.wait_ge(product_ready, UNITS_PER_STEP * (step + 1))
                for q in range(UNITS_PER_STEP):
                    rows = slice(0, P) if UNITS[unit_of(step, q)][0] == "full" else slice(EMB, P)
                    for chunk in range(2):
                        s = 2 * q + chunk
                        last = matmul(row_sums[32 * s:32 * s + 32, half, :], columns[rows],
                                      products[rows, step % PRODUCT_SLOTS, s, :],
                                      start=position == 0, stop=position == POSITIONS - 1,
                                      tile_position=(rows.start, 32 * s))
                last.then_inc(step_reduced, 1)

            def make_head_bias():
                pe.wait_ge(head_inputs_loaded, 16 * 4)
                for t in range(H1_TILES):
                    for part in range(2):
                        last = matmul(row_sums[:, 0, t:t + 1], w_top1_sb[:, part, P * t:P * (t + 1)],
                                      b_rec_sb[:, part:part + 1], start=part == 0, stop=part == 1)
                last.then_inc(head_bias_made, 1)

            def make_head_weights(tile, made):
                pe.wait_ge(head_inputs_loaded, 16 * 4)
                if made == 2:
                    pe.wait_ge(head_bias_ready, 1)
                if made > 2:
                    pe.wait_ge(head_weights_ready, made - 2)
                for part in range(2):
                    last = matmul(row_sums[:, tile % 2, :], w_rows_sb[:, part, P * tile:P * (tile + 1)],
                                  w_top1_sb[:, part, :], start=part == 0, stop=part == 1)
                last.then_inc(head_weights_made, 1)

            def look_up(k, first=0, last=ONE_HOT_TILES):
                if k >= OPENING_LOOKUPS:
                    pe.wait_ge(field_split, SPLIT_PARTS * arrival(ONE_HOT_FIELDS[k]))
                elif k >= UNITS_PER_STEP:
                    pe.wait_ge(field_split, SPLIT_PARTS * (arrival(ONE_HOT_FIELDS[k - UNITS_PER_STEP]) + 1))
                pe.wait_ge(table_rest_ready, k + 1)
                for tile in range(first, last):
                    made = ONE_HOT_TILES * k + tile
                    pe.wait_ge(one_hot_made, made + 1)
                    for half in range(HALVES):
                        cols = slice(HALF * half, HALF * (half + 1))
                        product = matmul(looked_up(k)[:, cols],
                                         table_parts[0:ONE_HOT_PARTS, k % TABLE_SLOTS, tile, :],
                                         one_hot[0:ONE_HOT_PARTS, made % ONE_HOT_SLOTS, cols],
                                         start=tile == 0, stop=tile == ONE_HOT_TILES - 1)
                    product.then_inc(one_hot_used, 1)

            def take_field(field):
                g = GATHERED_FIELDS.index(field)
                lookups = [arrival(f) for f in ONE_HOT_FIELDS[OPENING_LOOKUPS:] if arrival(f) < arrival(field)]
                if g >= 2:
                    previous = max([arrival(GATHERED_FIELDS[g - 2])] + lookups)
                    pe.wait_ge(field_split, SPLIT_PARTS * (previous + 1))
                pe.wait_ge(field_gathered[g % GATHER_SLOTS], 16 * B_TILES * (g // GATHER_SLOTS + 1))
                for t in range(B_TILES // 2):
                    two_tiles = gathered[:, g % GATHER_SLOTS, 2 * t:2 * t + 2, :].rearrange("p t e -> p (t e)")
                    last = nc.tensor.transpose(transposed(field)[:, P * t:P * (t + 1)], two_tiles,
                                               identity_sb[:, :])
                last.then_inc(field_transposed, 1)

            look_up(0)
            look_up(1)
            pe.wait_ge(identity_loaded, 16)
            take_field(FIELD_ORDER[1])
            make_head_bias()
            make_head_weights(3, 1)
            make_head_weights(2, 2)
            take_field(FIELD_ORDER[3])
            look_up(2)
            make_head_weights(1, 3)
            take_field(FIELD_ORDER[5])
            look_up(3)
            make_head_weights(0, 4)
            pe.wait_ge(selector_ready, 1)
            pe.wait_ge(field_split, SPLIT_PARTS * (arrival(ONE_HOT_FIELDS[OPENING_LOOKUPS - 1]) + 1))

            for step in range(STEPS):
                for event, field, parts in field_events[step]:
                    if event == "look up":
                        look_up(ONE_HOT_FIELDS.index(field), 4 * parts[0], 4 * parts[0] + 4)
                    if event == "take":
                        take_field(field)
                half = step % HALVES
                cols = slice(HALF * half, HALF * (half + 1))
                for q in range(UNITS_PER_STEP):
                    u = unit_of(step, q)
                    group = u // GROUP_UNITS
                    kslot = group % KERNEL_SLOTS
                    pe.wait_ge(kernel_rest_ready, group + 1)
                    pe.wait_ge(field_split, SPLIT_PARTS * (max(arrival(f) for f in unit_fields(UNITS[u])) + 1))
                    if step > 0:
                        pe.wait_ge(product_ready, UNITS_PER_STEP * (step - 1) + q + 1)
                    for chunk in range(2):
                        mslot = arrival(unit_fields(UNITS[u])[chunk]) % MOVING_SLOTS
                        at = (2 * (u % GROUP_UNITS) + chunk) * P
                        for part, kernel_part in enumerate((kernel_high, kernel_rest)):
                            last = matmul(inner[q][:, chunk, :], kernel_part[:, kslot, at:at + P],
                                          moving[:, mslot, cols], start=part == 0, stop=part == 1)
                    last.then_inc(inner_ready, 1)
                if step == 1:
                    pe.wait_ge(head_weights_ready, ROW_TILES)
                if step > 0:
                    reduce(step - 1)
            reduce(STEPS - 1)

            pe.wait_ge(weights_loaded, 16 * (3 + len(LONE_UNITS)))
            pe.wait_ge(product_ready, UNITS_PER_STEP * STEPS)
            for half in range(HALVES):
                cols = slice(HALF * half, HALF * (half + 1))
                for tile in range(ROW_TILES):
                    if half == 1 or tile == ROW_TILES - 1:
                        pe.wait_ge(sums_ready, HALVES * (ROW_TILES - 1) + (HALVES if half else 1))
                    for t in range(H1_TILES):
                        last = matmul(h1_banks(half)[t], w_head[:, tile, P * t:P * (t + 1)],
                                      sums[:, tile, cols], start=tile == 0, stop=tile == ROW_TILES - 1)
                last.then_inc(h1_made, 1)
            for half in range(HALVES):
                cols = slice(HALF * half, HALF * (half + 1))
                pe.wait_ge(h1_ready, half + 1)
                for t in range(H2_TILES):
                    for part in range(H1_TILES):
                        last = matmul(h2_banks(half)[t], w_top2_sb[:, part, P * t:P * (t + 1)],
                                      h1[:, part, cols], start=part == 0, stop=part == H1_TILES - 1)
                last.then_inc(h2_made, 1)
            pe.wait_ge(h2_ready, HALVES)
            for part in range(H2_TILES):
                for quarter in range(4):
                    cols = slice(BATCH // 4 * quarter, BATCH // 4 * (quarter + 1))
                    last = matmul(y_part(quarter), w_top3_sb[:, part:part + 1], h2[:, part, cols],
                                  start=part == 0, stop=part == H2_TILES - 1,
                                  tile_position=(0, 32 * quarter))
            last.then_inc(y_made, 1)


def lay_out(inputs):
    import numpy as np

    arrays = {}
    ids = np.asarray(inputs["ids"])
    arrays["ids"] = np.ascontiguousarray(
        ids.reshape(B_TILES, P, FIELDS).transpose(1, 0, 2).reshape(P, B_TILES * FIELDS))
    arrays["ids_t"] = np.ascontiguousarray(ids.T)
    arrays["one_hot_row"] = np.arange(ONE_HOT_ROWS, dtype=np.float32).reshape(ONE_HOT_PARTS, ONE_HOT_TILES)
    for f in range(FIELDS):
        arrays[f"tbl_{f}"] = np.ascontiguousarray(inputs[f"tbl_{f}"])
    by_pair = np.asarray(inputs["L0_rec_kernel"]).transpose(1, 2, 0)
    w = np.asarray(inputs["L0_rec_W"])
    stream = np.empty((len(UNITS), 2, 2, EMB, EMB), by_pair.dtype)
    w_rows = np.zeros((Z_DIM, ROWS), w.dtype)
    for u, unit in enumerate(UNITS):
        for chunk, field in enumerate(unit_fields(unit)):
            for parity in range(2):
                second = 2 * unit[2] + parity if unit[0] == "full" else field + 1
                p = pair_index(field, second)
                stream[u, chunk, parity] = by_pair[p] if field < second else by_pair[p].T
                if unit[0] == "full" or parity == 1:
                    w_rows[:, row_of(u, chunk, parity)] = w[:, p]
    arrays["kernel_stream"] = np.ascontiguousarray(
        stream.reshape(GROUPS, GROUP_UNITS * 4, EMB, EMB).transpose(0, 2, 1, 3).reshape(GROUPS, EMB, GROUP_COLS))
    arrays["w_rows"] = w_rows
    arrays["w_top1"] = np.ascontiguousarray(inputs["W_top1"])
    arrays["b_rec"] = np.ascontiguousarray(np.asarray(inputs["L0_rec_b"]).reshape(-1, P).T)
    arrays["b_top1"] = np.ascontiguousarray(np.asarray(inputs["b_top1"]).reshape(-1, P).T)
    arrays["w_top2"] = np.ascontiguousarray(inputs["W_top2"])
    arrays["b_top2"] = np.ascontiguousarray(np.asarray(inputs["b_top2"]).reshape(-1, P).T)
    arrays["w_top3"] = np.ascontiguousarray(np.asarray(inputs["W_top3"]).reshape(-1, P).T)
    arrays["dense_t"] = np.ascontiguousarray(np.asarray(inputs["dense_ctx"]).T)
    arrays["identity"] = np.eye(P, dtype=np.float32)
    return arrays


def kernel(**inputs):
    import numpy as np
    import concourse.bacc as bacc
    from concourse.bass_utils import run_bass_kernel_spmd

    nc = bacc.Bacc("TRN2", target_bir_lowering=False, num_devices=1)
    arrays, aps = {}, {}
    for name, a in lay_out(inputs).items():
        arrays[f"in_{name}"] = a
        aps[name] = nc.dram_tensor(f"in_{name}", a.shape, mybir.dt.from_np(a.dtype), kind="ExternalInput").ap()
    out = nc.dram_tensor("out_y", (BATCH, 1), mybir.dt.float32, kind="ExternalOutput").ap()
    tables = [aps.pop(f"tbl_{f}") for f in range(FIELDS)]
    dlrm_tower(nc, aps.pop("ids"), tables=tables, out=out, **aps)
    return run_bass_kernel_spmd(nc, [arrays], core_ids=[0]).results[0]["out_y"]
```
